# Optimizing a Trainium2 kernel written in Bass

```python
import numpy as np
import jax
import jax.numpy as jnp

def _softmax(x, axis=-1):
    return jax.nn.softmax(x, axis=axis)

def _gelu(x):
    return jax.nn.gelu(x, approximate=True)

def _silu(x):
    return jax.nn.silu(x)

def _sigmoid(x):
    return jax.nn.sigmoid(x)

def _layernorm(x, axis=-1, eps=1e-05):
    m = jnp.mean(x, axis=axis, keepdims=True)
    v = jnp.var(x, axis=axis, keepdims=True)
    return (x - m) / jnp.sqrt(v + eps)

def _scatter_add(tgt, idx, src, axis=0):
    return tgt.at[idx].add(src)

def _segment_sum(src, seg, n):
    return jax.ops.segment_sum(src, seg, n)
kernel_name = 'mk_seq_postln_d1_jaxref_r8_bc137d'

def setup_inputs(seed: int=0):
    np.random.seed(seed)
    _w = jnp.asarray

    def _L0_attn_setup():
        import jax, jax.numpy as jnp
        import numpy as np
        DIM = 128
        EXPAND = 1.5
        D_INNER = int(EXPAND * DIM)
        B, L = (4, 512)

        def _forward(x, W_in, W_out, conv_w, conv_b, dt_w, dt_b, A, Dp):
            xz = jnp.einsum('bld,ed->ble', x, W_in)
            x_inner, z = jnp.split(xz, 2, axis=-1)
            xc = jnp.transpose(x_inner, (0, 2, 1))
            xc = jax.lax.conv_general_dilated(xc, conv_w, window_strides=(1,), padding=[(1, 1)], dimension_numbers=('NCH', 'OIH', 'NCH'), feature_group_count=D_INNER)
            xc = xc + conv_b[None, :, None]
            x_conv = jax.nn.silu(jnp.transpose(xc, (0, 2, 1)))
            dt = jax.nn.softplus(jnp.einsum('blc,ec->ble', x_conv, dt_w) + dt_b)
            A_exp = jnp.exp(A[None, None, :] * dt)
            x_weighted = x_conv * dt
            y = jnp.cumsum(x_weighted * A_exp, axis=1) * A_exp
            y = y + x_conv * Dp[None, None, :]
            y = y * jax.nn.silu(z)
            return jnp.einsum('blc,dc->bld', y, W_out)
        key = jax.random.key(seed)
        ks = jax.random.split(key, 9)
        x = jax.random.normal(ks[0], (B, L, DIM), dtype=jnp.float32)
        W_in = jax.random.normal(ks[1], (D_INNER * 2, DIM), dtype=jnp.float32) / np.sqrt(DIM)
        W_out = jax.random.normal(ks[2], (DIM, D_INNER), dtype=jnp.float32) / np.sqrt(D_INNER)
        conv_w = jax.random.normal(ks[3], (D_INNER, 1, 3), dtype=jnp.float32) / np.sqrt(3.0)
        conv_b = jax.random.normal(ks[4], (D_INNER,), dtype=jnp.float32) * 0.01
        dt_w = jax.random.normal(ks[5], (D_INNER, D_INNER), dtype=jnp.float32) / np.sqrt(D_INNER)
        dt_b = jnp.zeros((D_INNER,), dtype=jnp.float32)
        A = -jax.random.uniform(ks[6], (D_INNER,), dtype=jnp.float32) * 0.1
        Dp = jnp.ones((D_INNER,), dtype=jnp.float32)
        return {'x': x, 'W_in': W_in, 'W_out': W_out, 'conv_w': conv_w, 'conv_b': conv_b, 'dt_w': dt_w, 'dt_b': dt_b, 'A': A, 'Dp': Dp}
    _L0_attn_in = _L0_attn_setup()

    def _L0_ffn_setup():
        import jax, jax.numpy as jnp
        import numpy as np
        from jax import lax
        D_MODEL = 128
        INTER = 128
        N_EXPERTS = 8
        TOP_K = 2
        ROUTE_SCALE = 1.0
        B, S = (2, 512)
        key = jax.random.key(seed)
        ks = jax.random.split(key, 16)
        sc_d = 1.0 / np.sqrt(D_MODEL)
        sc_f = 1.0 / np.sqrt(INTER)
        inp = {'x': jax.random.normal(ks[0], (B, S, D_MODEL), dtype=jnp.float32), 'gate_w': jax.random.normal(ks[1], (N_EXPERTS, D_MODEL), dtype=jnp.float32) * sc_d, 'w1': jax.random.normal(ks[2], (N_EXPERTS, D_MODEL, INTER), dtype=jnp.float32) * sc_d, 'b1': jnp.zeros((N_EXPERTS, INTER), dtype=jnp.float32), 'w2': jax.random.normal(ks[3], (N_EXPERTS, INTER, D_MODEL), dtype=jnp.float32) * sc_f, 'b2': jnp.zeros((N_EXPERTS, D_MODEL), dtype=jnp.float32), 'w3': jax.random.normal(ks[4], (N_EXPERTS, D_MODEL, INTER), dtype=jnp.float32) * sc_d, 'b3': jnp.zeros((N_EXPERTS, INTER), dtype=jnp.float32), 'sw1': jax.random.normal(ks[5], (D_MODEL, INTER), dtype=jnp.float32) * sc_d, 'sb1': jnp.zeros((INTER,), dtype=jnp.float32), 'sw2': jax.random.normal(ks[6], (INTER, D_MODEL), dtype=jnp.float32) * sc_f, 'sb2': jnp.zeros((D_MODEL,), dtype=jnp.float32), 'sw3': jax.random.normal(ks[7], (D_MODEL, INTER), dtype=jnp.float32) * sc_d, 'sb3': jnp.zeros((INTER,), dtype=jnp.float32)}
        return inp
    _L0_ffn_in = _L0_ffn_setup()
    _d = {'L0_attn_x': _L0_attn_in['x'], 'L0_attn_W_in': _L0_attn_in['W_in'], 'L0_attn_W_out': _L0_attn_in['W_out'], 'L0_attn_conv_w': _L0_attn_in['conv_w'], 'L0_attn_conv_b': _L0_attn_in['conv_b'], 'L0_attn_dt_w': _L0_attn_in['dt_w'], 'L0_attn_dt_b': _L0_attn_in['dt_b'], 'L0_attn_A': _L0_attn_in['A'], 'L0_attn_Dp': _L0_attn_in['Dp'], 'L0_ffn_gate_w': _L0_ffn_in['gate_w'], 'L0_ffn_w1': _L0_ffn_in['w1'], 'L0_ffn_b1': _L0_ffn_in['b1'], 'L0_ffn_w2': _L0_ffn_in['w2'], 'L0_ffn_b2': _L0_ffn_in['b2'], 'L0_ffn_w3': _L0_ffn_in['w3'], 'L0_ffn_b3': _L0_ffn_in['b3'], 'L0_ffn_sw1': _L0_ffn_in['sw1'], 'L0_ffn_sb1': _L0_ffn_in['sb1'], 'L0_ffn_sw2': _L0_ffn_in['sw2'], 'L0_ffn_sb2': _L0_ffn_in['sb2'], 'L0_ffn_sw3': _L0_ffn_in['sw3'], 'L0_ffn_sb3': _L0_ffn_in['sb3']}
    _x0 = _d['L0_attn_x']
    _d['L0_attn_x'] = jax.random.normal(jax.random.fold_in(jax.random.key(seed), 1), (4, 1024, 128), dtype=_x0.dtype)
    del _x0
    return _d

def reference(L0_attn_x, L0_attn_W_in, L0_attn_W_out, L0_attn_conv_w, L0_attn_conv_b, L0_attn_dt_w, L0_attn_dt_b, L0_attn_A, L0_attn_Dp, L0_ffn_gate_w, L0_ffn_w1, L0_ffn_b1, L0_ffn_w2, L0_ffn_b2, L0_ffn_w3, L0_ffn_b3, L0_ffn_sw1, L0_ffn_sb1, L0_ffn_sw2, L0_ffn_sb2, L0_ffn_sw3, L0_ffn_sb3):

    def _L0_attn_ref(x, W_in, W_out, conv_w, conv_b, dt_w, dt_b, A, Dp):
        import jax, jax.numpy as jnp
        import numpy as np
        DIM = 128
        EXPAND = 1.5
        D_INNER = int(EXPAND * DIM)
        B, L = (4, 512)

        def _forward(x, W_in, W_out, conv_w, conv_b, dt_w, dt_b, A, Dp):
            xz = jnp.einsum('bld,ed->ble', x, W_in)
            x_inner, z = jnp.split(xz, 2, axis=-1)
            xc = jnp.transpose(x_inner, (0, 2, 1))
            xc = jax.lax.conv_general_dilated(xc, conv_w, window_strides=(1,), padding=[(1, 1)], dimension_numbers=('NCH', 'OIH', 'NCH'), feature_group_count=D_INNER)
            xc = xc + conv_b[None, :, None]
            x_conv = jax.nn.silu(jnp.transpose(xc, (0, 2, 1)))
            dt = jax.nn.softplus(jnp.einsum('blc,ec->ble', x_conv, dt_w) + dt_b)
            A_exp = jnp.exp(A[None, None, :] * dt)
            x_weighted = x_conv * dt
            y = jnp.cumsum(x_weighted * A_exp, axis=1) * A_exp
            y = y + x_conv * Dp[None, None, :]
            y = y * jax.nn.silu(z)
            return jnp.einsum('blc,dc->bld', y, W_out)
        return _forward(x, W_in, W_out, conv_w, conv_b, dt_w, dt_b, A, Dp)

    def _L0_ffn_ref(x, gate_w, w1, b1, w2, b2, w3, b3, sw1, sb1, sw2, sb2, sw3, sb3):
        import jax, jax.numpy as jnp
        import numpy as np
        from jax import lax
        D_MODEL = 128
        INTER = 128
        N_EXPERTS = 8
        TOP_K = 2
        ROUTE_SCALE = 1.0
        B, S = (2, 512)
        Bx, Sx, D = x.shape
        xt = x.reshape(-1, D)
        scores = jax.nn.softmax((xt @ gate_w.T).astype(jnp.float32), axis=-1)
        top_vals, top_idx = lax.top_k(scores, TOP_K)
        weights = (top_vals * ROUTE_SCALE).astype(x.dtype)
        combine = jnp.sum(jax.nn.one_hot(top_idx, N_EXPERTS, dtype=x.dtype) * weights[..., None], axis=1)

        def body(acc, p):
            W1, B1, W2, B2, W3, B3, c = p
            h = jax.nn.silu(xt @ W1 + B1) * (xt @ W3 + B3)
            return (acc + c[:, None] * (h @ W2 + B2), None)
        y, _ = lax.scan(body, jnp.zeros_like(xt), (w1, b1, w2, b2, w3, b3, combine.T))
        z = jax.nn.silu(xt @ sw1 + sb1) * (xt @ sw3 + sb3) @ sw2 + sb2
        return (y + z).reshape(Bx, Sx, D)
    x = L0_attn_x
    x = _layernorm(x + _L0_attn_ref(x, L0_attn_W_in, L0_attn_W_out, L0_attn_conv_w, L0_attn_conv_b, L0_attn_dt_w, L0_attn_dt_b, L0_attn_A, L0_attn_Dp), axis=-1)
    x = _layernorm(x + _L0_ffn_ref(x, L0_ffn_gate_w, L0_ffn_w1, L0_ffn_b1, L0_ffn_w2, L0_ffn_b2, L0_ffn_w3, L0_ffn_b3, L0_ffn_sw1, L0_ffn_sb1, L0_ffn_sw2, L0_ffn_sb2, L0_ffn_sw3, L0_ffn_sb3), axis=-1)
    return x

_drawn_inputs = setup_inputs


def setup_inputs(seed=0):
    import zlib

    import numpy as np

    out = dict(_drawn_inputs(seed))
    spreads = {'L0_attn_dt_b': (0.0, 0.1),
     'L0_attn_Dp': (1.0, 0.6),
     'L0_ffn_b1': (0.0, 0.371),
     'L0_ffn_b2': (0.0, 0.1),
     'L0_ffn_b3': (0.0, 0.373),
     'L0_ffn_sb1': (0.0, 0.1),
     'L0_ffn_sb2': (0.0, 0.1),
     'L0_ffn_sb3': (0.0, 0.1)}
    factors = {}
    for name, (base, spread) in spreads.items():
        noise = np.random.default_rng([zlib.crc32(name.encode()), seed]).standard_normal(out[name].shape)
        drawn = base * np.exp(spread * noise) if base else spread * noise
        out[name] = jnp.asarray(drawn.astype(out[name].dtype))
    for name, factor in factors.items():
        out[name] = (out[name] * factor).astype(out[name].dtype)
    return out
```

```python
from contextlib import ExitStack

import numpy as np
import concourse.bass as bass
from concourse import mybir

ALU = mybir.AluOpType
ACT = mybir.ActivationFunctionType
F32 = mybir.dt.float32
F32R = mybir.dt.float32r

P = 128
T = 512
NCH = T // P
EPS = 1e-5
DT_CLAMP = 40.0
W0, W1, W2, CB, DTB, AC, DP = range(7)


def build(nc, x, xT, w_in, w_out, w_dt, chan, gate, w1, w3, w2, b1, b3, b2, sb2, out):
    tokens = x.shape[0]
    NB = tokens // T
    DI = w_out.shape[0]
    CR = DI - P
    NE = gate.shape[1]
    NX = NE + 1
    LAST = NB - 1
    rows = (P, CR)

    x_chunks = x.rearrange("(b c p) d -> b p c d", c=NCH, p=P)
    out_chunks = out.rearrange("(b c p) d -> b p c d", c=NCH, p=P)

    with ExitStack() as ctx:
        def sb(name, shape, dt=F32):
            return ctx.enter_context(nc.sbuf_tensor(name, shape, dt))

        def bank(name):
            return ctx.enter_context(nc.psum_tensor(name, [P, T], F32))

        def sem(name):
            return ctx.enter_context(nc.semaphore(name))

        win_raw = sb("win_raw", [P, 2 * DI])
        win_h, win_l = sb("win_h", [P, 2 * DI], F32R), sb("win_l", [P, 2 * DI], F32R)
        wdt = sb("wdt", [P, 2, 2 * P])
        wout = sb("wout", [P, 2, P])
        cv = sb("cv", [P, 2, 7])
        wgate = sb("wgate", [P, NE])
        w13_raw = sb("w13_raw", [P, 2, NX, P])
        w13_h, w13_l = sb("w13_h", [P, 2, NX, P], F32R), sb("w13_l", [P, 2, NX, P], F32R)
        w2_sb = sb("w2_sb", [P, NX, P])
        b13 = sb("b13", [P, 2, NX])
        b2_raw = sb("b2_raw", [P, P])
        b2_h, b2_l = sb("b2_h", [P, P], F32R), sb("b2_l", [P, P], F32R)
        ident = sb("ident", [P, P])
        pick_raw = sb("pick_raw", [P, NE, P])
        pick = sb("pick", [P, NE, P], F32R)
        zeros = sb("zeros", [P, T])
        group_keep = sb("group_keep", [P, NCH * NE])
        euler = sb("euler", [P, NCH * NE])
        minus_half = sb("minus_half", [P, NCH])

        xw = sb("xw", [P, 2, T + 2])
        xh, xl = sb("xh", [P, 2, T + 2], F32R), sb("xl", [P, 2, T + 2], F32R)
        craw = sb("craw", [P, 2, T + 2])
        tap = sb("tap", [P, 2, T])
        conv = sb("conv", [P, 2, T])
        xconv = sb("xconv", [P, 2, 2, T])
        sz = sb("sz", [P, 2, 2, T])
        soft = sb("soft", [P, 2, T])
        dt = sb("dt", [P, 2, 2, T])
        ae = sb("ae", [P, 2, 2, T])
        x_tm = sb("x_tm", [P, 2, NCH, P])
        csum = sb("csum", [P, 2, 2, T])
        y = sb("y", [P, 2, T])
        r = sb("r", [P, NCH, P])
        stats = sb("stats", [P, NCH, 6])
        mv = sb("mv", [P, NCH, 2])
        ve = sb("ve", [P, NCH])
        rstd = sb("rstd", [P, NCH])
        x1T = sb("x1T", [P, 2, T])
        x1h, x1l = sb("x1h", [P, 2, T], F32R), sb("x1l", [P, 2, T], F32R)
        lg = sb("lg", [P, NCH, NE])
        top = sb("top", [P, NCH, 8])
        shifted = sb("shifted", [P, NCH, NE])
        ex = sb("ex", [P, NCH, NE])
        above, level, order, wanted = (sb(n, [P, NCH, NE]) for n in ("above", "level", "order", "wanted"))
        n_above = sb("n_above", [P, NCH])
        den, rden = sb("den", [P, NCH]), sb("rden", [P, NCH])
        comb = sb("comb", [P, NCH, P])
        cT = sb("cT", [P, 2, T], F32R)
        s_act = sb("s_act", [P, 2, T])
        hu = sb("hu", [P, T])
        h = sb("h", [P, 3, T])
        fin = sb("fin", [P, T])
        stats2 = sb("stats2", [P, NCH, 6])
        mv2 = sb("mv2", [P, NCH, 2])
        ve2 = sb("ve2", [P, NCH])
        rstd2 = sb("rstd2", [P, NCH])
        o_tm = sb("o_tm", [P, 2, NCH, P])

        bG, bU, bC, bY, m0, m1, m2, m3 = (bank(n) for n in ("bG", "bU", "bC", "bY", "m0", "m1", "m2", "m3"))

        ld_win, ld_small, ld_w13, ld_w2, ld_b2 = (sem(n) for n in ("ld_win", "ld_small", "ld_w13", "ld_w2", "ld_b2"))
        z_window, z_pool, z_dve = sem("z_window"), sem("z_pool"), sem("z_dve")
        c_ident, c_pickraw = sem("c_ident"), sem("c_pickraw")
        c_winh, c_winl, c_w13h, c_w13l, c_pick, c_b2h, c_b2l = (
            sem(n) for n in ("c_winh", "c_winl", "c_w13h", "c_w13l", "c_pick", "c_b2h", "c_b2l"))
        xw_in = [sem("xw_in0"), sem("xw_in1")]
        x_in = [sem("x_in0"), sem("x_in1")]
        o_out = [sem("o_out0"), sem("o_out1")]
        (f_xh, f_xl, f_proj, f_raw, f_cv, f_sx, f_B, f_sz, f_dtm, f_v, f_e, f_L, f_dt, f_ae) = (
            sem(n) for n in ("f_xh", "f_xl", "f_proj", "f_raw", "f_cv", "f_sx", "f_B", "f_sz", "f_dtm", "f_v",
                             "f_e", "f_L", "f_dt", "f_ae"))
        (s_wd, s_g, s_cs, s_y1, s_y2, s_y, s_op, s_r, s_bn, s_mv, s_ve, s_rs, s_x1, s_xt, s_x1h, s_x1l, s_lg,
         s_l, s_d, s_ex, s_gate, s_cc, s_ct, s_cT) = (
            sem(n) for n in ("s_wd", "s_g", "s_cs", "s_y1", "s_y2", "s_y", "s_op", "s_r", "s_bn", "s_mv", "s_ve",
                             "s_rs", "s_x1", "s_xt", "s_x1h", "s_x1l", "s_lg", "s_l", "s_d", "s_ex", "s_gate",
                             "s_cc", "s_ct", "s_cT"))
        (e_g, e_u, e_cb, e_s, e_hu, e_h, e_y, e_yd, e_f, n_t, n_bn, n_mv, n_ve, n_rs, n_o) = (
            sem(n) for n in ("e_g", "e_u", "e_cb", "e_s", "e_hu", "e_h", "e_y", "e_yd", "e_f", "n_t", "n_bn",
                             "n_mv", "n_ve", "n_rs", "n_o"))

        def wait(eng, s, v):
            if not (isinstance(v, int) and v <= 0):
                eng.wait_ge(s, v)

        block = ctx.enter_context(nc.Block())

        @block.sync
        def _(sp):
            sp.dma_start(win_raw[:], w_in).then_inc(ld_win, 16)

            def load_window(j):
                p = j % 2
                wait(sp, f_xl, j - 1)
                if j == 0 or j == 1:
                    sp.wait_ge(z_window, 1)
                if p == 0:
                    dst, src = xw[:, p, 1:T + 2], xT[:, j * T:(j + 1) * T + 1]
                else:
                    dst, src = xw[:, p, 0:T + 1], xT[:, j * T - 1:(j + 1) * T]
                sp.dma_start(dst, src).then_inc(xw_in[p], 16)

            load_window(0)
            sp.dma_start(cv[:, 0, :], chan[0:P, :]).then_inc(ld_small, 16)
            sp.dma_start(cv[0:CR, 1, :], chan[P:DI, :]).then_inc(ld_small, 16)
            sp.wait_ge(z_dve, 1)
            sp.dma_start(wdt[:, 0, 0:DI], w_dt[0:P, :]).then_inc(ld_small, 16)
            sp.dma_start(wdt[0:CR, 1, 0:DI], w_dt[P:DI, :]).then_inc(ld_small, 16)
            sp.dma_start(wout[:, 0, :], w_out[0:P, :]).then_inc(ld_small, 16)
            sp.dma_start(wout[0:CR, 1, :], w_out[P:DI, :]).then_inc(ld_small, 16)
            sp.dma_start(wgate[:], gate).then_inc(ld_small, 16)
            sp.dma_start(b13[:, 0, :], b1).then_inc(ld_small, 16)
            sp.dma_start(b13[:, 1, :], b3).then_inc(ld_small, 16)
            load_window(1)
            for j in range(2):
                sp.dma_start(x_tm[:, j], x_chunks[j]).then_inc(x_in[j], 16)
            sp.dma_start(w13_raw[:, 0], w1).then_inc(ld_w13, 16)
            sp.dma_start(w13_raw[:, 1], w3).then_inc(ld_w13, 16)
            sp.dma_start(w2_sb[:], w2).then_inc(ld_w2, 16)
            sp.wait_ge(z_pool, 1)
            sp.dma_start(b2_raw[0:NE, :], b2).then_inc(ld_b2, 16)
            sp.dma_start(b2_raw[NE:2 * NE, :], b2).then_inc(ld_b2, 16)
            sp.dma_start(b2_raw[2 * NE:2 * NE + 1, :], sb2).then_inc(ld_b2, 16)

            for s in range(NB + 3):
                j = s + 2
                if j < NB:
                    load_window(j)
                j = s + 1
                if 2 <= j < NB:
                    wait(sp, s_r, j - 1)
                    sp.dma_start(x_tm[:, j % 2], x_chunks[j]).then_inc(x_in[j % 2], 16)
                j = s - 3
                if j >= 0:
                    sp.wait_ge(n_o, j + 1)
                    sp.dma_start(out_chunks[j], o_tm[:, j % 2]).then_inc(o_out[j % 2], 16)
            for p in range(2):
                sp.wait_ge(o_out[p], 16 * NB // 2)

        @block.tensor
        def _(pe):
            def mm3(dst, wh, wl, mh, ml, start=True, stop=True):
                pe.matmul(dst, wh, mh, start=start, stop=False)
                pe.matmul(dst, wh, ml, start=False, stop=False)
                return pe.matmul(dst, wl, mh, start=False, stop=stop)

            def f_project(j):
                p = j % 2
                if j == 0:
                    pe.wait_ge(c_winl, 1)
                pe.wait_ge(f_xl, j + 1)
                for t, dst in ((0, m0), (1, m1)):
                    wait(pe, f_dt, 2 * (j - 1) + t + 1)
                    c = slice(t * P, (t + 1) * P)
                    mm3(dst[:], win_h[:, c], win_l[:, c], xh[:, p, 1:T + 1], xl[:, p, 1:T + 1]).then_inc(f_proj, 1)
                wait(pe, s_l, j - 1)
                for t in range(2):
                    c = slice(t * P, (t + 1) * P)
                    last = mm3(m2[:, 2 * t:2 * t + 2], win_h[:, c], win_l[:, c],
                               xh[:, p, 0:T + 2:T + 1], xl[:, p, 0:T + 2:T + 1])
                last.then_inc(f_proj, 1)

            def f_project_z(j):
                p = j % 2
                pe.wait_ge(f_raw, 2 * j + 2)
                c = slice(2 * P, 3 * P)
                mm3(m2[:], win_h[:, c], win_l[:, c], xh[:, p, 1:T + 1], xl[:, p, 1:T + 1]).then_inc(f_B, 1)

            def f_dt_product(j):
                p = j % 2
                if j == 0:
                    pe.wait_ge(ld_small, 9 * 16)
                    pe.wait_ge(z_dve, 2)
                pe.wait_ge(f_sx, 2 * j + 2)
                pe.wait_ge(f_sz, 2 * j + 1)
                for t, dst in ((0, m0), (1, m1)):
                    c = slice(t * P, (t + 1) * P)
                    pe.matmul(dst[:], wdt[:, 0, c], xconv[:, p, 0], start=True, stop=False)
                    pe.matmul(dst[:], wdt[:, 1, c], xconv[:, p, 1], start=False, stop=True).then_inc(f_dtm, 1)

            def s_project(j):
                pe.wait_ge(s_y, 2 * j + 2)
                pe.wait_ge(f_sz, min(2 * (j + 2), 2 * NB))
                for c in range(NCH):
                    k = slice(c * P, (c + 1) * P)
                    pe.matmul(m2[:, k], y[:, 0, k], wout[:, 0, :], start=True, stop=False)
                    last = pe.matmul(m2[:, k], y[:, 1, k], wout[:, 1, :], start=False, stop=True)
                last.then_inc(s_op, 1)

            def s_turn(j):
                pe.wait_ge(s_x1, j + 1)
                wait(pe, n_o, j - 1)
                for c in range(NCH):
                    k = slice(c * P, (c + 1) * P)
                    last = pe.transpose(m3[:, k], r[:, c, :], ident[:])
                last.then_inc(s_xt, 1)

            def s_route(j):
                p = j % 2
                pe.wait_ge(s_x1h, j + 1)
                pe.wait_ge(s_r, j + 1)
                for c in range(NCH):
                    last = pe.matmul(m2[:, c * NE:(c + 1) * NE], x1T[:, p, c * P:(c + 1) * P], wgate[:],
                                     start=True, stop=True)
                last.then_inc(s_lg, 1)

            def s_turn_weights(j):
                pe.wait_ge(s_cc, j + 1)
                for c in range(NCH):
                    k = slice(c * P, (c + 1) * P)
                    last = pe.transpose(m3[:, k], comb[:, c, :], ident[:])
                last.then_inc(s_ct, 1)

            def e_up(j, k):
                p = j % 2
                e = (k - 1) % NX
                if j == 0 and k == 0:
                    pe.wait_ge(c_w13l, 1)
                if k == 0:
                    pe.wait_ge(s_x1l, j + 1)
                wait(pe, e_s, NX * j + k)
                mm3(bG[:], w13_h[:, 0, e], w13_l[:, 0, e], x1h[:, p], x1l[:, p]).then_inc(e_g, 1)
                wait(pe, e_hu, NX * j + k)
                mm3(bU[:], w13_h[:, 1, e], w13_l[:, 1, e], x1h[:, p], x1l[:, p]).then_inc(e_u, 1)
                if k >= 1:
                    if k == 1:
                        pe.wait_ge(s_cT, j + 1)
                    if j == 0 and k == 1:
                        pe.wait_ge(c_pick, 1)
                    wait(pe, e_h, NE * j + k - 1)
                    pe.matmul(bC[:], pick[:, e], cT[:, p], start=True, stop=True).then_inc(e_cb, 1)

            def e_down(j, k):
                e = (k - 1) % NX
                if k == 0:
                    pe.wait_ge(e_hu, NX * j + 1)
                    wait(pe, e_f, j)
                    if j == 0:
                        pe.wait_ge(ld_w2, 16)
                else:
                    pe.wait_ge(e_h, NE * j + k)
                pe.matmul(bY[:], w2_sb[:, e], h[:, k % 3], start=(k == 0), stop=False).then_inc(e_y, 1)

            def e_bias(j):
                p = j % 2
                if j == 0:
                    pe.wait_ge(c_b2l, 1)
                pe.matmul(bY[:], b2_h[:], cT[:, p], start=False, stop=False)
                pe.matmul(bY[:], b2_l[:], cT[:, p], start=False, stop=True).then_inc(e_yd, 1)

            def n_turn(j):
                pe.wait_ge(e_f, j + 1)
                pe.wait_ge(s_cT, min(j + 2, NB))
                for c in range(NCH):
                    k = slice(c * P, (c + 1) * P)
                    last = pe.transpose(m3[:, k], fin[:, k], ident[:])
                last.then_inc(n_t, 1)

            pe.wait_ge(c_ident, 1)
            for s in range(NB + 3):
                F, S, E, N = s < NB, 1 <= s <= NB, 2 <= s <= NB + 1, s >= 3
                if E:
                    e_up(s - 2, 0)
                if N:
                    n_turn(s - 3)
                if E:
                    e_up(s - 2, 1)
                if F:
                    f_project(s)
                if E:
                    e_up(s - 2, 2)
                    e_down(s - 2, 0)
                if F:
                    f_project_z(s)
                if E:
                    e_up(s - 2, 3)
                    e_down(s - 2, 1)
                    e_up(s - 2, 4)
                    e_down(s - 2, 2)
                if F:
                    f_dt_product(s)
                if E:
                    e_up(s - 2, 5)
                    e_down(s - 2, 3)
                if S:
                    s_project(s - 1)
                if E:
                    e_up(s - 2, 6)
                    e_down(s - 2, 4)
                    e_up(s - 2, 7)
                    e_down(s - 2, 5)
                if S:
                    s_turn(s - 1)
                if E:
                    e_up(s - 2, 8)
                    e_down(s - 2, 6)
                if S:
                    s_route(s - 1)
                if E:
                    e_down(s - 2, 7)
                    e_down(s - 2, 8)
                    e_bias(s - 2)
                if S:
                    s_turn_weights(s - 1)

        @block.scalar
        def _(act):
            def split_window(j):
                p = j % 2
                act.wait_ge(xw_in[p], 16 * (j // 2 + 1))
                wait(act, f_B, j - 1)
                act.activation(xh[:, p], xw[:, p], ACT.Copy).then_inc(f_xh, 1)

            def f_taps(j):
                p = j % 2
                if j == 0:
                    act.wait_ge(ld_small, 9 * 16)
                act.wait_ge(f_proj, 3 * j + 3)
                wait(act, f_cv, 4 * j)
                for t, src in ((0, m0), (1, m1)):
                    n = rows[t]
                    act.activation(craw[0:n, t, 1:T + 1], src[0:n, :], ACT.Copy)
                    act.activation(craw[0:n, t, 0:T + 2:T + 1], m2[0:n, 2 * t:2 * t + 2], ACT.Copy)
                    act.activation(tap[0:n, t], src[0:n, :], ACT.Identity, scale=cv[0:n, t, W1:W1 + 1],
                                   bias=cv[0:n, t, CB:CB + 1]).then_inc(f_raw, 1)
                wait(act, s_y, 2 * (j - 1))
                act.activation(sz[0:CR, p, 1], m1[CR:2 * CR, :], ACT.Silu).then_inc(f_sz, 1)

            def f_silu(j):
                p = j % 2
                for t in range(2):
                    n = rows[t]
                    act.wait_ge(f_cv, 4 * j + 3 + t)
                    if j == 0 and t == 1:
                        act.wait_ge(z_dve, 2)
                    act.activation(xconv[0:n, p, t], conv[0:n, t], ACT.Silu).then_inc(f_sx, 1)
                act.wait_ge(f_B, j + 1)
                act.activation(sz[:, p, 0], m2[:], ACT.Silu).then_inc(f_sz, 1)

            def f_softplus(j):
                p = j % 2
                act.preload_act_table_set("natural_log_exp_and_others")
                for t in range(2):
                    n = rows[t]
                    act.wait_ge(f_v, 2 * j + t + 1)
                    act.activation(soft[0:n, t], soft[0:n, t], ACT.Exp).then_inc(f_e, 1)
                for t in range(2):
                    n = rows[t]
                    act.wait_ge(f_e, 2 * j + t + 1)
                    act.activation(soft[0:n, t], soft[0:n, t], ACT.Ln, bias=1.0).then_inc(f_L, 1)
                for t in range(2):
                    n = rows[t]
                    act.wait_ge(f_dt, 2 * j + t + 1)
                    act.activation(ae[0:n, p, t], dt[0:n, p, t], ACT.Exp,
                                   scale=cv[0:n, t, AC:AC + 1]).then_inc(f_ae, 1)

            def s_copy(j):
                p = j % 2
                act.wait_ge(s_xt, j + 1)
                wait(act, e_f, j - 1)
                act.activation(x1T[:, p], m3[:], ACT.Copy)
                act.activation(x1h[:, p], m3[:], ACT.Copy).then_inc(s_x1h, 1)

            def s_copy_weights(j):
                p = j % 2
                act.wait_ge(s_ct, j + 1)
                wait(act, e_yd, j - 1)
                act.activation(cT[:, p], m3[:], ACT.Copy).then_inc(s_cT, 1)

            def e_silu(j, k):
                e = (k - 1) % NX
                act.wait_ge(e_g, NX * j + k + 1)
                wait(act, e_hu, NX * j + k - 1)
                act.activation(s_act[:, k % 2], bG[:], ACT.Silu, bias=b13[:, 0, e:e + 1]).then_inc(e_s, 1)

            act.wait_ge(ld_win, 16)
            act.activation(win_h[:], win_raw[:], ACT.Copy).then_inc(c_winh, 1)
            split_window(0)
            for s in range(NB + 2):
                F, S, E = s < NB, 1 <= s <= NB, s >= 2
                if E:
                    e_silu(s - 2, 0)
                    e_silu(s - 2, 1)
                if F:
                    f_taps(s)
                if E:
                    e_silu(s - 2, 2)
                if F:
                    f_silu(s)
                if E:
                    e_silu(s - 2, 3)
                    e_silu(s - 2, 4)
                if F:
                    f_softplus(s)
                if s == 0:
                    act.wait_ge(ld_w13, 32)
                    act.activation(w13_h[:].rearrange("p a e d -> p (a e d)"),
                                   w13_raw[:].rearrange("p a e d -> p (a e d)"), ACT.Copy).then_inc(c_w13h, 1)
                    act.wait_ge(c_pickraw, 2)
                    act.activation(pick[:].rearrange("p e d -> p (e d)"),
                                   pick_raw[:].rearrange("p e d -> p (e d)"), ACT.Copy).then_inc(c_pick, 1)
                    act.wait_ge(ld_b2, 48)
                    act.activation(b2_h[:], b2_raw[:], ACT.Copy).then_inc(c_b2h, 1)
                if E:
                    e_silu(s - 2, 5)
                    e_silu(s - 2, 6)
                    e_silu(s - 2, 7)
                if s + 1 < NB:
                    split_window(s + 1)
                if S:
                    s_copy(s - 1)
                if E:
                    e_silu(s - 2, 8)
                if S:
                    s_copy_weights(s - 1)

        @block.vector
        def _(dve):
            gates = [0]

            def f_conv(j):
                wait(dve, f_sx, 2 * j)
                for t in range(2):
                    n = rows[t]
                    dve.wait_ge(f_raw, 2 * j + t + 1)
                    wait(dve, f_cv, 4 * j)
                    dve.scalar_tensor_tensor(out=conv[0:n, t], in0=craw[0:n, t, 0:T], scalar=cv[0:n, t, W0:W0 + 1],
                                             in1=tap[0:n, t], op0=ALU.mult, op1=ALU.add).then_inc(f_cv, 1)
                for t in range(2):
                    n = rows[t]
                    dve.wait_ge(f_cv, 4 * j + t + 1)
                    dve.scalar_tensor_tensor(out=conv[0:n, t], in0=craw[0:n, t, 2:T + 2],
                                             scalar=cv[0:n, t, W2:W2 + 1], in1=conv[0:n, t],
                                             op0=ALU.mult, op1=ALU.add).then_inc(f_cv, 1)

            def f_soft(j):
                p = j % 2
                for t, src in ((0, m0), (1, m1)):
                    n = rows[t]
                    dve.wait_ge(f_dtm, 2 * j + t + 1)
                    wait(dve, f_dt, 2 * (j - 1) + t + 1)
                    dve.tensor_scalar(soft[0:n, t], src[0:n, :], cv[0:n, t, DTB:DTB + 1], DT_CLAMP,
                                      ALU.add, ALU.min).then_inc(f_v, 1)
                for t, src in ((0, m0), (1, m1)):
                    n = rows[t]
                    dve.wait_ge(f_L, 2 * j + t + 1)
                    wait(dve, s_g, 2 * (j - 2) + t + 1)
                    dve.scalar_tensor_tensor(out=dt[0:n, p, t], in0=src[0:n, :], scalar=cv[0:n, t, DTB:DTB + 1],
                                             in1=soft[0:n, t], op0=ALU.add, op1=ALU.max).then_inc(f_dt, 1)

            def s_sum(j, t):
                p, n = j % 2, rows[t]
                dve.wait_ge(s_g, 2 * j + t + 1)
                wait(dve, s_cs, 2 * (j - 1) + t + 1)
                first = 0.0 if p == 0 else csum[0:n, 1 - p, t, T - 1:T]
                dve.tensor_tensor_scan(csum[0:n, p, t], dt[0:n, p, t], zeros[0:n], first,
                                       ALU.add, ALU.add).then_inc(s_cs, 1)
                dve.wait_ge(s_cs, 2 * j + t + 1)
                dve.tensor_tensor(ae[0:n, p, t], csum[0:n, p, t], ae[0:n, p, t], ALU.mult).then_inc(s_y1, 1)
                dve.wait_ge(s_y1, 2 * j + t + 1)
                dve.scalar_tensor_tensor(out=ae[0:n, p, t], in0=xconv[0:n, p, t], scalar=cv[0:n, t, DP:DP + 1],
                                         in1=ae[0:n, p, t], op0=ALU.mult, op1=ALU.add).then_inc(s_y2, 1)

            def s_stats(j):
                p = j % 2
                dve.wait_ge(s_op, j + 1)
                dve.wait_ge(x_in[p], 16 * (j // 2 + 1))
                wait(dve, s_xt, j)
                flat = r[:].rearrange("p c d -> p (c d)")
                dve.tensor_tensor(flat, m2[:], x_tm[:, p].rearrange("p c d -> p (c d)"), ALU.add).then_inc(s_r, 1)
                dve.wait_ge(s_r, j + 1)
                for c in range(NCH):
                    last = dve.bn_stats(stats[:, c], r[:, c])
                last.then_inc(s_bn, 1)
                dve.wait_ge(s_bn, j + 1)
                for c in range(NCH):
                    last = dve.bn_aggr(mv[:, c], stats[:, c])
                last.then_inc(s_mv, 1)

            def s_norm(j):
                dve.wait_ge(s_rs, j + 1)
                for c in range(NCH):
                    last = dve.tensor_scalar(r[:, c], r[:, c], mv[:, c, 0:1], rstd[:, c:c + 1],
                                             ALU.subtract, ALU.mult)
                last.then_inc(s_x1, 1)

            def step(ins):
                gates[0] += 1
                ins.then_inc(s_gate, 1)
                dve.wait_ge(s_gate, gates[0])

            def s_gating(j):
                dve.wait_ge(s_lg, j + 1)
                flat = lambda t: t[:].rearrange("p c e -> p (c e)")
                dve.tensor_copy(flat(lg), m2[:, 0:NCH * NE]).then_inc(s_l, 1)
                dve.wait_ge(s_l, j + 1)
                for c in range(NCH):
                    last = dve.max(top[:, c], lg[:, c])
                step(last)
                best = top[:, :, 0:1].broadcast_to([P, NCH, NE])
                second = top[:, :, 1:2].broadcast_to([P, NCH, NE])
                dve.tensor_tensor(shifted[:], lg[:], best, ALU.subtract).then_inc(s_d, 1)
                dve.tensor_tensor(above[:], lg[:], second, ALU.is_gt)
                dve.tensor_tensor(n_above[:], top[:, :, 0], top[:, :, 1], ALU.is_gt)
                step(dve.tensor_tensor(level[:], lg[:], second, ALU.is_equal))
                step(dve.tensor_tensor_scan(flat(order), group_keep[:], flat(level), 0.0, ALU.mult, ALU.add))
                step(dve.tensor_tensor(order[:], order[:], n_above[:].unsqueeze(2).broadcast_to([P, NCH, NE]), ALU.add))
                step(dve.scalar_tensor_tensor(out=flat(wanted), in0=flat(order), scalar=2.0, in1=flat(level),
                                              op0=ALU.is_le, op1=ALU.mult))
                step(dve.tensor_tensor(wanted[:], wanted[:], above[:], ALU.add))
                dve.wait_ge(s_ex, j + 1)
                dve.tensor_tensor(wanted[:], wanted[:], ex[:], ALU.mult)
                step(dve.tensor_reduce(den[:], ex[:], mybir.AxisListType.X, ALU.add))
                step(dve.reciprocal(rden[:], den[:]))
                step(dve.tensor_tensor(wanted[:], wanted[:], rden[:].unsqueeze(2).broadcast_to([P, NCH, NE]), ALU.mult))
                wait(dve, s_ct, j)
                step(dve.tensor_copy(comb[:, :, 0:NE].bitcast(F32R), wanted[:]))
                dve.tensor_tensor(comb[:, :, NE:2 * NE].bitcast(F32R), wanted[:], comb[:, :, 0:NE],
                                  ALU.subtract).then_inc(s_cc, 1)

            def e_hidden(j, k):
                e = (k - 1) % NX
                dve.wait_ge(e_s, NX * j + k + 1)
                dve.wait_ge(e_u, NX * j + k + 1)
                wait(dve, e_h, NE * j + k - 1 if k else NE * j)
                if k == 0:
                    wait(dve, e_y, NX * j - 2)
                dve.scalar_tensor_tensor(out=h[:, 0] if k == 0 else hu[:], in0=bU[:], scalar=b13[:, 1, e:e + 1],
                                         in1=s_act[:, k % 2], op0=ALU.add, op1=ALU.mult).then_inc(e_hu, 1)
                if k:
                    dve.wait_ge(e_hu, NX * j + k + 1)
                    dve.wait_ge(e_cb, NE * j + k)
                    wait(dve, e_y, NX * j + k - 2)
                    dve.tensor_tensor(h[:, k % 3], hu[:], bC[:], ALU.mult).then_inc(e_h, 1)

            def e_sum(j):
                dve.wait_ge(e_yd, j + 1)
                wait(dve, n_t, j)
                dve.tensor_tensor(fin[:], bY[:], x1T[:, j % 2], ALU.add).then_inc(e_f, 1)

            def n_stats(j):
                dve.wait_ge(n_t, j + 1)
                for c in range(NCH):
                    last = dve.bn_stats(stats2[:, c], m3[:, c * P:(c + 1) * P])
                last.then_inc(n_bn, 1)
                dve.wait_ge(n_bn, j + 1)
                for c in range(NCH):
                    last = dve.bn_aggr(mv2[:, c], stats2[:, c])
                last.then_inc(n_mv, 1)

            def n_norm(j):
                p = j % 2
                dve.wait_ge(n_rs, j + 1)
                wait(dve, o_out[p], 16 * (j // 2))
                for c in range(NCH):
                    last = dve.tensor_scalar(o_tm[:, p, c], m3[:, c * P:(c + 1) * P], mv2[:, c, 0:1],
                                             rstd2[:, c:c + 1], ALU.subtract, ALU.mult)
                last.then_inc(n_o, 1)

            dve.memset(wdt[:], 0.0)
            dve.memset(wout[:], 0.0).then_inc(z_dve, 1)
            dve.memset(xconv[CR:P, :, 1], 0.0)
            dve.memset(y[CR:P, 1], 0.0)
            dve.memset(zeros[:], 0.0)
            dve.memset(comb[:], 0.0)
            dve.memset(group_keep[:], 1.0).then_inc(z_dve, 1)
            dve.wait_ge(z_dve, 2)
            dve.memset(group_keep[:, 0:NCH * NE:NE], 0.0)
            dve.memset(comb[:, :, 2 * NE:2 * NE + 1], 1.0).then_inc(z_dve, 1)
            dve.wait_ge(c_winh, 1)
            dve.tensor_tensor(win_l[:], win_raw[:], win_h[:].bitcast(F32), ALU.subtract).then_inc(c_winl, 1)
            dve.wait_ge(ld_small, 9 * 16)
            dve.wait_ge(z_dve, 3)
            for s in range(NB + 3):
                F, S, E, N = s < NB, 1 <= s <= NB, 2 <= s <= NB + 1, s >= 3
                if N:
                    e_sum(s - 3)
                if E:
                    e_hidden(s - 2, 0)
                if N:
                    n_stats(s - 3)
                if E:
                    e_hidden(s - 2, 1)
                if S:
                    s_sum(s - 1, 0)
                if N:
                    n_norm(s - 3)
                if F:
                    f_conv(s)
                if E:
                    e_hidden(s - 2, 2)
                if S:
                    s_sum(s - 1, 1)
                if E:
                    e_hidden(s - 2, 3)
                    e_hidden(s - 2, 4)
                if F:
                    f_soft(s)
                if E:
                    e_hidden(s - 2, 5)
                if S:
                    s_stats(s - 1)
                if E:
                    e_hidden(s - 2, 6)
                if S:
                    s_norm(s - 1)
                if E:
                    e_hidden(s - 2, 7)
                    e_hidden(s - 2, 8)
                if S:
                    s_gating(s - 1)

        @block.gpsimd
        def _(pool):
            def split_low(j):
                p = j % 2
                pool.wait_ge(f_xh, j + 1)
                wait(pool, f_B, j - 1)
                pool.tensor_tensor(xl[:, p], xw[:, p], xh[:, p].bitcast(F32), ALU.subtract).then_inc(f_xl, 1)

            def s_weigh(j, t):
                p, n = j % 2, rows[t]
                pool.wait_ge(f_ae, 2 * j + t + 1)
                pool.tensor_tensor(dt[0:n, p, t], dt[0:n, p, t], xconv[0:n, p, t], ALU.mult).then_inc(s_wd, 1)
                pool.wait_ge(s_wd, 2 * j + t + 1)
                pool.tensor_tensor(dt[0:n, p, t], dt[0:n, p, t], ae[0:n, p, t], ALU.mult).then_inc(s_g, 1)

            def s_z(j, t):
                p, n = j % 2, rows[t]
                pool.wait_ge(s_y2, 2 * j + t + 1)
                wait(pool, s_op, j)
                if j == 0:
                    pool.wait_ge(z_dve, 2)
                pool.tensor_tensor(y[0:n, t], ae[0:n, p, t], sz[0:n, p, t], ALU.mult).then_inc(s_y, 1)

            def inv_std(j, have, mean_var, shifted_var, eps_done, result, done):
                pool.wait_ge(have, j + 1)
                pool.tensor_scalar(shifted_var[:], mean_var[:, :, 1], EPS, 1.0, ALU.add, ALU.mult).then_inc(eps_done, 1)
                pool.wait_ge(eps_done, j + 1)
                pool.tensor_tensor(result[:], shifted_var[:], minus_half[:], ALU.pow).then_inc(done, 1)

            def s_low(j):
                p = j % 2
                pool.wait_ge(s_x1h, j + 1)
                wait(pool, e_yd, j - 1)
                pool.tensor_tensor(x1l[:, p], x1T[:, p], x1h[:, p].bitcast(F32), ALU.subtract).then_inc(s_x1l, 1)

            def s_exp(j):
                pool.wait_ge(s_d, j + 1)
                pool.tensor_tensor(ex[:].rearrange("p c e -> p (c e)"), euler[:],
                                   shifted[:].rearrange("p c e -> p (c e)"), ALU.pow).then_inc(s_ex, 1)

            pool.memset(xw[:, :, 0:T + 2:T + 1], 0.0).then_inc(z_window, 1)
            pool.memset(ident[:], 0.0)
            pool.memset(pick_raw[:], 0.0)
            pool.memset(b2_raw[:], 0.0)
            pool.memset(euler[:], float(np.e))
            pool.memset(minus_half[:], -0.5).then_inc(z_pool, 1)
            pool.wait_ge(z_pool, 1)
            pool.affine_select(out=ident[:], in_=ident[:], compare_op=ALU.not_equal, fill=1.0, base=0,
                               pattern=[[-1, P]], channel_multiplier=1).then_inc(c_ident, 1)
            pool.affine_select(out=pick_raw[:], in_=pick_raw[:], compare_op=ALU.not_equal, fill=1.0, base=0,
                               pattern=[[-1, NE], [0, P]], channel_multiplier=1).then_inc(c_pickraw, 1)
            pool.wait_ge(c_pickraw, 1)
            pool.affine_select(out=pick_raw[:], in_=pick_raw[:], compare_op=ALU.not_equal, fill=1.0, base=-NE,
                               pattern=[[-1, NE], [0, P]], channel_multiplier=1).then_inc(c_pickraw, 1)
            split_low(0)
            for s in range(NB + 3):
                F, S, E, N = s < NB, 1 <= s <= NB, 2 <= s <= NB + 1, s >= 3
                if S:
                    s_weigh(s - 1, 0)
                if N:
                    inv_std(s - 3, n_mv, mv2, ve2, n_ve, rstd2, n_rs)
                if S:
                    s_weigh(s - 1, 1)
                    s_z(s - 1, 0)
                    s_z(s - 1, 1)
                if s + 1 < NB:
                    split_low(s + 1)
                if s == 0:
                    pool.wait_ge(c_w13h, 1)
                    pool.tensor_tensor(w13_l[:].rearrange("p a e d -> p (a e d)"),
                                       w13_raw[:].rearrange("p a e d -> p (a e d)"),
                                       w13_h[:].bitcast(F32).rearrange("p a e d -> p (a e d)"),
                                       ALU.subtract).then_inc(c_w13l, 1)
                    pool.wait_ge(c_b2h, 1)
                    pool.tensor_tensor(b2_l[:], b2_raw[:], b2_h[:].bitcast(F32), ALU.subtract).then_inc(c_b2l, 1)
                if S:
                    inv_std(s - 1, s_mv, mv, ve, s_ve, rstd, s_rs)
                    s_low(s - 1)
                    s_exp(s - 1)


def kernel(**inputs):
    import concourse.bacc as bacc
    from concourse.bass_utils import run_bass_kernel_spmd

    i = {k.replace("L0_", ""): np.asarray(v) for k, v in inputs.items()}
    B, L, D = i["attn_x"].shape
    DI = i["attn_W_out"].shape[1]
    x = i["attn_x"].reshape(B * L, D)
    w_in = i["attn_W_in"]
    w_in = np.concatenate([w_in[:P], w_in[P:DI], w_in[DI + P:], w_in[DI:DI + P]])
    stack = lambda routed, shared: np.concatenate([i[routed], i[shared][None]]).swapaxes(0, 1)
    arrays = {
        "x": x,
        "xT": x.T,
        "w_in": w_in.T,
        "w_out": i["attn_W_out"].T,
        "w_dt": i["attn_dt_w"].T,
        "chan": np.stack([*i["attn_conv_w"][:, 0].T, i["attn_conv_b"], i["attn_dt_b"], i["attn_A"], i["attn_Dp"]], 1),
        "gate": i["ffn_gate_w"].T,
        "w1": stack("ffn_w1", "ffn_sw1"),
        "w3": stack("ffn_w3", "ffn_sw3"),
        "w2": stack("ffn_w2", "ffn_sw2"),
        "b1": stack("ffn_b1", "ffn_sb1"),
        "b3": stack("ffn_b3", "ffn_sb3"),
        "b2": i["ffn_b2"],
        "sb2": i["ffn_sb2"][None],
    }
    arrays = {f"{k}_dram": np.ascontiguousarray(v) for k, v in arrays.items()}
    nc = bacc.Bacc("TRN2", target_bir_lowering=False, num_devices=1)
    args = [nc.dram_tensor(k, a.shape, mybir.dt.from_np(a.dtype), kind="ExternalInput").ap()
            for k, a in arrays.items()]
    out = nc.dram_tensor("out_dram", (B * L, D), F32, kind="ExternalOutput").ap()
    build(nc, *args, out)
    got = run_bass_kernel_spmd(nc, [arrays], core_ids=[0]).results[0]["out_dram"]
    return got.reshape(B, L, D)
```

```python
from contextlib import ExitStack

import numpy as np
import concourse.bass as bass
from concourse import mybir

ALU = mybir.AluOpType
ACT = mybir.ActivationFunctionType
F32 = mybir.dt.float32
F32R = mybir.dt.float32r

P = 128
T = 512
NCH = T // P
EPS = 1e-5
TOP = 32
LEAD = 3
W0, W1, W2, CB, DTB, AC, DP = range(7)
SPLIT = ()


def build(nc, x, xT, w_in, small, w_dt, w_out_gate, w13, w2, b2, out):
    tokens = x.shape[0]
    NB = tokens // T
    DI = w_in.shape[1] // 2
    CR = DI - P
    NX = w2.shape[1]
    NE = NX - 1
    LAST = NB - 1
    rows = (P, CR)

    x_chunks = x.rearrange("(b c p) d -> b p c d", c=NCH, p=P)
    out_chunks = out.rearrange("(b c p) d -> b p c d", c=NCH, p=P)

    with ExitStack() as ctx:
        def sb(name, shape, dt=F32):
            return ctx.enter_context(nc.sbuf_tensor(name, shape, dt))

        def bank(name):
            return ctx.enter_context(nc.psum_tensor(name, [P, T], F32))

        def sem(name):
            return ctx.enter_context(nc.semaphore(name))

        win_raw = sb("win_raw", [P, 2 * DI])
        win_h, win_l = sb("win_h", [P, 2 * DI], F32R), sb("win_l", [P, 2 * DI], F32R)
        wdt_raw = sb("wdt_raw", [P, 2, 2 * P])
        wdt_h, wdt_l = sb("wdt_h", [P, 2, 2 * P], F32R), sb("wdt_l", [P, 2, 2 * P], F32R)
        wout_gate = sb("wout_gate", [P, 2 * P + NE])
        wout, wgate = wout_gate[:, 0:2 * P].rearrange("p (t d) -> p t d", t=2), wout_gate[:, 2 * P:]
        small_sb = sb("small_sb", [P, 2 * 7 + 2 * NX])
        cv = small_sb[:, 0:14].rearrange("p (t c) -> p t c", t=2)
        b13 = small_sb[:, 14:].rearrange("p (a e) -> p a e", a=2)
        w13_raw = sb("w13_raw", [P, 2, NX, P])
        w13_h, w13_l = sb("w13_h", [P, 2, NX, P], F32R), sb("w13_l", [P, 2, NX, P], F32R)
        w2_sb = sb("w2_sb", [P, NX, P])
        b2_raw = sb("b2_raw", [P, P])
        b2_hl = sb("b2_hl", [P, P], F32R)
        w2_h, w2_l = sb("w2_h", [P, NX, P], F32R), sb("w2_l", [P, NX, P], F32R)
        h_h, h_l = sb("h_h", [P, 2, T], F32R), sb("h_l", [P, 2, T], F32R)
        ident = sb("ident", [P, P])
        pick_raw = sb("pick_raw", [P, NE, P])
        pick = sb("pick", [P, NE, P], F32R)
        zeros = sb("zeros", [P, T])
        group_keep = sb("group_keep", [P, NCH * NE])
        minus_half = sb("minus_half", [P, NCH])

        xw = sb("xw", [P, 2, T + 2])
        xh, xl = sb("xh", [P, 2, T + 2], F32R), sb("xl", [P, 2, T + 2], F32R)
        craw = sb("craw", [P, 2, T + 2])
        tap = sb("tap", [P, 2, T])
        conv = sb("conv", [P, 2, T])
        xconv = sb("xconv", [P, 2, 2, T])
        sz = sb("sz", [P, 2, 2, T])
        xc_h = sb("xc_h", [P, 2, 2, T], F32R)
        xc_l = sb("xc_l", [P, 2, T], F32R)
        mag = sb("mag", [P, 2, T])
        pos = sb("pos", [P, 2, T])
        dt = sb("dt", [P, 2, 2, T])
        ae = sb("ae", [P, 2, 2, T])
        x_tm = sb("x_tm", [P, 2, NCH, P])
        csum = sb("csum", [P, 2, 2, T])
        y = sb("y", [P, 2, T])
        r = sb("r", [P, NCH, P])
        stats = sb("stats", [P, NCH, 6])
        mv = sb("mv", [P, NCH, 2])
        ve = sb("ve", [P, NCH])
        rstd = sb("rstd", [P, NCH])
        x1T = sb("x1T", [P, 2, T])
        x1h, x1l = sb("x1h", [P, 2, T], F32R), sb("x1l", [P, 2, T], F32R)
        lg = sb("lg", [P, NCH, NE])
        top = sb("top", [P, NCH, 8])
        shifted = sb("shifted", [P, NCH, NE])
        ex = sb("ex", [P, NCH, NE])
        above, level, order, wanted = (sb(n, [P, NCH, NE]) for n in ("above", "level", "order", "wanted"))
        n_above = sb("n_above", [P, NCH])
        den, rden = sb("den", [P, NCH]), sb("rden", [P, NCH])
        comb = sb("comb", [P, NCH, P])
        cT = sb("cT", [P, 2, T], F32R)
        s_act = sb("s_act", [P, 2, T])
        hu = sb("hu", [P, 2, T])
        h = sb("h", [P, 3, T])
        fin = sb("fin", [P, T])
        stats2 = sb("stats2", [P, NCH, 6])
        mv2 = sb("mv2", [P, NCH, 2])
        ve2 = sb("ve2", [P, NCH])
        rstd2 = sb("rstd2", [P, NCH])
        neg_mean = sb("neg_mean", [P, NCH])
        shift2 = sb("shift2", [P, NCH])
        o_tm = sb("o_tm", [P, 2, NCH, P])

        bG, bU, bC, bY, m0, m1, m2, m3 = (bank(n) for n in ("bG", "bU", "bC", "bY", "m0", "m1", "m2", "m3"))

        ld_win, ld_small, ld_wdt, ld_wout, ld_w13, ld_w2, ld_b2 = (
            sem(n) for n in ("ld_win", "ld_small", "ld_wdt", "ld_wout", "ld_w13", "ld_w2", "ld_b2"))
        z_window, z_pool, z_dve = sem("z_window"), sem("z_pool"), sem("z_dve")
        c_ident, c_pickraw = sem("c_ident"), sem("c_pickraw")
        c_winh, c_winl, c_wdth, c_wdtl, c_w13h, c_w13l, c_pick, c_b2h, c_b2l = (
            sem(n) for n in ("c_winh", "c_winl", "c_wdth", "c_wdtl", "c_w13h", "c_w13l", "c_pick", "c_b2h", "c_b2l"))
        xw_in = [sem("xw_in0"), sem("xw_in1")]
        x_in = [sem("x_in0"), sem("x_in1")]
        o_out = [sem("o_out0"), sem("o_out1")]
        (f_xh, f_xl, f_proj, f_raw, f_cv, f_sx, f_lowA, f_lowC, f_B, f_szC, f_szA, f_dtm, f_v, f_e, f_L, f_dt,
         f_ae) = (
            sem(n) for n in ("f_xh", "f_xl", "f_proj", "f_raw", "f_cv", "f_sx", "f_lowA", "f_lowC", "f_B", "f_szC",
                             "f_szA", "f_dtm", "f_v", "f_e", "f_L", "f_dt", "f_ae"))
        (s_wd, s_g, s_cs, s_y1, s_y2, s_y, s_op, s_r, s_bn, s_mv, s_ve, s_rs, s_x1, s_xt, s_x1h, s_x1l, s_lg,
         s_l, s_d, s_ex, s_gate, s_cc, s_ct, s_cT, s_ch) = (
            sem(n) for n in ("s_wd", "s_g", "s_cs", "s_y1", "s_y2", "s_y", "s_op", "s_r", "s_bn", "s_mv", "s_ve",
                             "s_rs", "s_x1", "s_xt", "s_x1h", "s_x1l", "s_lg", "s_l", "s_d", "s_ex", "s_gate",
                             "s_cc", "s_ct", "s_cT", "s_ch"))
        (e_g, e_u, e_cb, e_s, e_hu, e_h, e_y, e_yd, e_f, n_t, n_bn, n_mv, n_ve, n_rs, n_sh, n_o) = (
            sem(n) for n in ("e_g", "e_u", "e_cb", "e_s", "e_hu", "e_h", "e_y", "e_yd", "e_f", "n_t", "n_bn",
                             "n_mv", "n_ve", "n_rs", "n_sh", "n_o"))

        c_w2h, c_w2l, e_hh, e_hl = sem("c_w2h"), sem("c_w2l"), sem("e_hh"), sem("e_hl")

        def wait(eng, s, v):
            if not (isinstance(v, int) and v <= 0):
                eng.wait_ge(s, v)

        block = ctx.enter_context(nc.Block())

        @block.sync
        def _(sp):
            sp.dma_start(win_raw[:], w_in).then_inc(ld_win, 16)

            def load_window(j):
                p = j % 2
                wait(sp, f_xl, j - 1)
                if j == 0 or j == 1:
                    sp.wait_ge(z_window, 1)
                if p == 0:
                    dst, src = xw[:, p, 1:T + 2], xT[:, j * T:(j + 1) * T + 1]
                else:
                    dst, src = xw[:, p, 0:T + 1], xT[:, j * T - 1:(j + 1) * T]
                sp.dma_start(dst, src).then_inc(xw_in[p], 16)

            load_window(0)
            sp.dma_start(small_sb[:], small).then_inc(ld_small, 16)
            sp.dma_start(wdt_raw[:].rearrange("p t d -> p (t d)"), w_dt).then_inc(ld_wdt, 16)
            load_window(1)
            sp.dma_start(w13_raw[:].rearrange("p a e d -> p (a e d)"), w13).then_inc(ld_w13, 16)
            sp.dma_start(wout_gate[:], w_out_gate).then_inc(ld_wout, 16)
            for j in range(2):
                sp.dma_start(x_tm[:, j], x_chunks[j]).then_inc(x_in[j], 16)
            sp.dma_start(w2_sb[:], w2).then_inc(ld_w2, 16)
            sp.dma_start(b2_raw[:], b2).then_inc(ld_b2, 16)

            for s in range(NB + 4):
                j = s + 2
                if j < NB:
                    load_window(j)
                j = s + 1
                if 2 <= j < NB:
                    wait(sp, s_r, j - 1)
                    sp.dma_start(x_tm[:, j % 2], x_chunks[j]).then_inc(x_in[j % 2], 16)
                j = s - 4
                if j >= 0:
                    sp.wait_ge(n_o, j + 1)
                    sp.dma_start(out_chunks[j], o_tm[:, j % 2]).then_inc(o_out[j % 2], 16)
            for p in range(2):
                sp.wait_ge(o_out[p], 16 * NB // 2)


        def once():
            ran = {}

            def do(piece, j, *which):
                if ran.get((piece, which), 0) == j < NB:
                    piece(j, *which)
                    ran[piece, which] = j + 1
            return do

        @block.tensor
        def _(pe):
            def mm3(dst, wh, wl, mh, ml, start=True, stop=True):
                pe.matmul(dst, wh, mh, start=start, stop=False)
                pe.matmul(dst, wh, ml, start=False, stop=False)
                return pe.matmul(dst, wl, mh, start=False, stop=stop)

            n = {"dt": 0, "z": 0, "sproj": 0, "proj": 0, "route": 0, "turn": 0, "turnw": 0, "nturn": 0}

            def project_in(j):
                p = j % 2
                if j == 0:
                    pe.wait_ge(c_winl, 1)
                pe.wait_ge(f_xl, j + 1)
                A, C, Z = (bG, bU, bC) if j == 1 else (m0, m1, m2)
                for t, dst in ((0, A), (1, C)):
                    if j != 1:
                        wait(pe, f_v, 2 * (n["dt"] - 1) + t + 1)
                        if t == 1:
                            wait(pe, s_r, n["sproj"])
                    c = slice(t * P, (t + 1) * P)
                    mm3(dst[:], win_h[:, c], win_l[:, c], xh[:, p, 1:T + 1], xl[:, p, 1:T + 1]).then_inc(f_proj, 1)
                if j != 1:
                    wait(pe, f_szA, n["z"])
                    wait(pe, s_l, n["route"])
                for t in range(2):
                    c = slice(t * P, (t + 1) * P)
                    last = mm3(Z[:, 2 * t:2 * t + 2], win_h[:, c], win_l[:, c],
                               xh[:, p, 0:T + 2:T + 1], xl[:, p, 0:T + 2:T + 1])
                last.then_inc(f_proj, 1)
                if j != 1:
                    n["proj"] = j + 1

            def project_z(j):
                p = j % 2
                if j != 1:
                    wait(pe, s_l, n["route"])
                pe.wait_ge(f_raw, 2 * j + 2)
                c = slice(2 * P, 3 * P)
                mm3((bC if j == 1 else m2)[:], win_h[:, c], win_l[:, c],
                    xh[:, p, 1:T + 1], xl[:, p, 1:T + 1]).then_inc(f_B, 1)
                if j != 1:
                    n["z"] = j + 1

            def project_dt(j):
                p = j % 2
                if j == 0:
                    pe.wait_ge(c_wdtl, 1)
                pe.wait_ge(f_sx, 2 * j + 2)
                pe.wait_ge(f_lowA, j + 1)
                pe.wait_ge(f_lowC, j + 1)
                pe.wait_ge(f_szC, j + 1)
                if j != 1:
                    wait(pe, s_r, n["sproj"])
                for t, dst in ((0, bG if j == 1 else m0), (1, bU if j == 1 else m1)):
                    c = slice(t * P, (t + 1) * P)
                    mm3(dst[:], wdt_h[:, 0, c], wdt_l[:, 0, c], xc_h[:, p, 0], xc_l[:, p], stop=False)
                    pe.matmul(dst[:], wdt_h[:, 1, c], xc_h[:, p, 1], start=False, stop=False)
                    pe.matmul(dst[:], wdt_l[:, 1, c], xc_h[:, p, 1], start=False, stop=True).then_inc(f_dtm, 1)
                if j != 1:
                    n["dt"] = j + 1

            def project_out(j):
                pe.wait_ge(s_y, 2 * j + 2)
                dst = bY if j == 0 else m1
                if j > 0:
                    wait(pe, f_v, 2 * n["dt"])
                    wait(pe, f_szC, n["proj"])
                if j == 0:
                    pe.wait_ge(ld_wout, 16)
                for c in range(NCH):
                    k = slice(c * P, (c + 1) * P)
                    pe.matmul(dst[:, k], y[:, 0, k], wout[:, 0, :], start=True, stop=False)
                    last = pe.matmul(dst[:, k], y[:, 1, k], wout[:, 1, :], start=False, stop=True)
                last.then_inc(s_op, 1)
                if j > 0:
                    n["sproj"] = j + 1

            def m3_free():
                wait(pe, s_x1h, n["turn"])
                wait(pe, s_cT, n["turnw"])
                wait(pe, n_o, n["nturn"])

            def turn_x1(j):
                pe.wait_ge(s_x1, j + 1)
                m3_free()
                for c in range(NCH):
                    k = slice(c * P, (c + 1) * P)
                    last = pe.transpose(m3[:, k], r[:, c, :], ident[:])
                last.then_inc(s_xt, 1)
                n["turn"] = j + 1

            def score_experts(j):
                p = j % 2
                pe.wait_ge(s_x1h, j + 1)
                pe.wait_ge(f_raw, 2 * n["proj"])
                pe.wait_ge(f_szA, n["z"])
                wait(pe, s_l, j)
                for c in range(NCH):
                    last = pe.matmul(m2[:, c * NE:(c + 1) * NE], x1T[:, p, c * P:(c + 1) * P], wgate,
                                     start=True, stop=True)
                last.then_inc(s_lg, 1)
                n["route"] = j + 1

            def turn_weights(j):
                pe.wait_ge(s_cc, j + 1)
                m3_free()
                for c in range(NCH):
                    k = slice(c * P, (c + 1) * P)
                    last = pe.transpose(m3[:, k], comb[:, c, :], ident[:])
                last.then_inc(s_ct, 1)
                n["turnw"] = j + 1

            def expert_g(j, k):
                p = j % 2
                e = (k - 1) % NX
                if j == 0 and k == 0:
                    pe.wait_ge(c_w13l, 1)
                    pe.wait_ge(f_v, 4)
                if k == 0:
                    pe.wait_ge(s_x1l, j + 1)
                wait(pe, e_s, NX * j + k)
                mm3(bG[:], w13_h[:, 0, e], w13_l[:, 0, e], x1h[:, p], x1l[:, p]).then_inc(e_g, 1)

            def expert_u(j, k):
                p = j % 2
                e = (k - 1) % NX
                wait(pe, e_hu, NX * j + k)
                mm3(bU[:], w13_h[:, 1, e], w13_l[:, 1, e], x1h[:, p], x1l[:, p]).then_inc(e_u, 1)

            def spread_weight(j, k):
                e = (k - 1) % NX
                if k == 1:
                    pe.wait_ge(s_cT, j + 1)
                    if j == 0:
                        pe.wait_ge(c_pick, 1)
                        pe.wait_ge(f_szA, 2)
                wait(pe, e_h, NE * j + k - 1)
                pe.matmul(bC[:], pick[:, e], cT[:, j % 2], start=True, stop=True).then_inc(e_cb, 1)

            def expert_down(j, k):
                e = (k - 1) % NX
                if k == 0:
                    pe.wait_ge(e_hu, NX * j + 1)
                    wait(pe, e_f, j)
                    if j == 0:
                        pe.wait_ge(ld_w2, 16)
                        pe.wait_ge(s_r, 1)
                elif k not in SPLIT:
                    pe.wait_ge(e_h, NE * j + k)
                if k in SPLIT:
                    i = len(SPLIT) * j + SPLIT.index(k)
                    if i == 0:
                        pe.wait_ge(c_w2l, 1)
                    pe.wait_ge(e_hl, i + 1)
                    mm3(bY[:], w2_h[:, e], w2_l[:, e], h_h[:, i % 2], h_l[:, i % 2],
                        start=(k == 0), stop=False).then_inc(e_y, 1)
                else:
                    pe.matmul(bY[:], w2_sb[:, e], h[:, k % 3], start=(k == 0), stop=False).then_inc(e_y, 1)

            def add_biases(j):
                p = j % 2
                if j == 0:
                    pe.wait_ge(c_b2l, 1)
                pe.matmul(bY[:], b2_hl[:], cT[:, p], start=False, stop=True).then_inc(e_yd, 1)

            def turn_sum(j):
                pe.wait_ge(e_f, j + 1)
                m3_free()
                for c in range(NCH):
                    k = slice(c * P, (c + 1) * P)
                    last = pe.transpose(m3[:, k], fin[:, k], ident[:])
                last.then_inc(n_t, 1)
                n["nturn"] = j + 1

            pe.wait_ge(c_ident, 1)
            do = once()
            do(project_in, 0)
            do(project_z, 0)
            do(project_in, 1)
            do(project_z, 1)
            do(project_dt, 0)
            do(project_dt, 1)
            do(project_in, 2)
            do(project_z, 2)
            do(project_out, 0)
            do(project_dt, 2)
            do(turn_x1, 0)
            do(expert_g, 0, 0)
            do(score_experts, 0)
            do(expert_u, 0, 0)
            do(project_out, 1)
            do(project_in, 3)
            do(turn_weights, 0)
            for s in range(LEAD, NB + 6):
                do(project_in, s)
                do(expert_g, s - 3, 0)
                do(expert_u, s - 3, 0)
                do(turn_x1, s - 2)
                do(expert_g, s - 3, 1)
                do(spread_weight, s - 3, 1)
                do(expert_u, s - 3, 1)
                do(expert_g, s - 3, 2)
                do(expert_down, s - 3, 0)
                do(expert_u, s - 3, 2)
                do(score_experts, s - 2)
                do(turn_sum, s - 4)
                do(expert_g, s - 3, 3)
                do(expert_u, s - 3, 3)
                do(spread_weight, s - 3, 2)
                do(expert_down, s - 3, 1)
                do(expert_g, s - 3, 4)
                do(project_dt, s)
                do(spread_weight, s - 3, 3)
                do(expert_u, s - 3, 4)
                do(expert_g, s - 3, 5)
                do(expert_down, s - 3, 2)
                do(spread_weight, s - 3, 4)
                do(expert_u, s - 3, 5)
                do(project_z, s)
                do(expert_g, s - 3, 6)
                do(expert_down, s - 3, 3)
                do(spread_weight, s - 3, 5)
                do(expert_u, s - 3, 6)
                do(expert_down, s - 3, 4)
                do(spread_weight, s - 3, 6)
                do(project_out, s - 1)
                do(expert_g, s - 3, 7)
                do(expert_u, s - 3, 7)
                do(expert_down, s - 3, 5)
                do(expert_g, s - 3, 8)
                do(spread_weight, s - 3, 7)
                do(expert_u, s - 3, 8)
                do(expert_down, s - 3, 6)
                do(spread_weight, s - 3, 8)
                do(expert_down, s - 3, 7)
                do(turn_weights, s - 2)
                do(expert_down, s - 3, 8)
                do(add_biases, s - 3)

        @block.scalar
        def _(act):
            def split_x(j):
                p = j % 2
                act.wait_ge(xw_in[p], 16 * (j // 2 + 1))
                wait(act, f_B, j - 1)
                act.activation(xh[:, p], xw[:, p], ACT.Copy).then_inc(f_xh, 1)

            def middle_tap(j, t):
                n = rows[t]
                src, Z = ((bG, bU)[t], bC) if j == 1 else ((m0, m1)[t], m2)
                if j == 0:
                    act.wait_ge(ld_small, 16)
                act.wait_ge(f_proj, 3 * j + 1 + t)
                wait(act, f_cv, 4 * (j - 1) + 2 * t + 2)
                act.activation(tap[0:n, t], src[0:n, :], ACT.Identity, scale=cv[0:n, t, W1:W1 + 1],
                               bias=cv[0:n, t, CB:CB + 1])
                act.activation(craw[0:n, t, 1:T + 1], src[0:n, :], ACT.Copy)
                act.wait_ge(f_proj, 3 * j + 3)
                act.activation(craw[0:n, t, 0:T + 2:T + 1], Z[0:n, 2 * t:2 * t + 2], ACT.Copy).then_inc(f_raw, 1)

            def silu_z_c(j):
                act.wait_ge(f_proj, 3 * j + 2)
                wait(act, s_y, 2 * (j - 1))
                act.activation(sz[0:CR, j % 2, 1], (bU if j == 1 else m1)[CR:2 * CR, :], ACT.Silu).then_inc(f_szC, 1)

            def silu_conv(j, t):
                p, n = j % 2, rows[t]
                wait(act, f_dtm, 2 * (j - 1))
                wait(act, s_y2, 2 * (j - 2) + t + 1)
                act.wait_ge(f_cv, 4 * j + 2 * t + 2)
                act.activation(xconv[0:n, p, t], conv[0:n, t], ACT.Silu)
                act.activation(xc_h[0:n, p, t], conv[0:n, t], ACT.Silu).then_inc(f_sx, 1)

            def silu_z_a(j):
                act.wait_ge(f_B, j + 1)
                wait(act, s_y, 2 * (j - 2) + 1)
                act.activation(sz[:, j % 2, 0], (bC if j == 1 else m2)[:], ACT.Silu).then_inc(f_szA, 1)

            def softplus_parts(j, t):
                src = (bG, bU)[t] if j == 1 else (m0, m1)[t]
                n, bias = rows[t], cv[0:rows[t], t, DTB:DTB + 1]
                act.wait_ge(f_dtm, 2 * j + t + 1)
                wait(act, f_dt, 2 * (j - 1) + t + 1)
                act.activation(mag[0:n, t], src[0:n, :], ACT.Abs, bias=bias)
                act.activation(pos[0:n, t], src[0:n, :], ACT.Relu, bias=bias).then_inc(f_v, 1)

            def load_ln_exp():
                act.preload_act_table_set("natural_log_exp_and_others")

            def softplus_exp(j, t):
                n = rows[t]
                act.wait_ge(f_v, 2 * j + t + 1)
                act.activation(mag[0:n, t], mag[0:n, t], ACT.Exp, scale=-1.0).then_inc(f_e, 1)

            def softplus_ln(j, t):
                n = rows[t]
                act.wait_ge(f_e, 2 * j + t + 1)
                act.activation(mag[0:n, t], mag[0:n, t], ACT.Ln, bias=1.0).then_inc(f_L, 1)

            def decay(j, t):
                p = j % 2
                n = rows[t]
                act.wait_ge(f_dt, 2 * j + t + 1)
                wait(act, s_y, 2 * (j - 2) + t + 1)
                act.activation(ae[0:n, p, t], dt[0:n, p, t], ACT.Exp,
                               scale=cv[0:n, t, AC:AC + 1]).then_inc(f_ae, 1)

            def exp_scores(j):
                act.wait_ge(s_d, j + 1)
                act.activation(ex[:], shifted[:], ACT.Exp).then_inc(s_ex, 1)

            def norm_sum(j):
                p = j % 2
                act.wait_ge(n_sh, j + 1)
                wait(act, o_out[p], 16 * (j // 2))
                for c in range(NCH):
                    last = act.activation(o_tm[:, p, c], m3[:, c * P:(c + 1) * P], ACT.Identity,
                                          scale=rstd2[:, c:c + 1], bias=shift2[:, c:c + 1])
                last.then_inc(n_o, 1)

            def copy_x1(j):
                p = j % 2
                act.wait_ge(s_xt, j + 1)
                wait(act, e_f, j - 1)
                act.activation(x1T[:, p], m3[:], ACT.Copy)
                act.activation(x1h[:, p], m3[:], ACT.Copy).then_inc(s_x1h, 1)

            def copy_weights(j):
                p = j % 2
                act.wait_ge(s_ct, j + 1)
                wait(act, e_yd, j - 1)
                act.activation(cT[:, p], m3[:], ACT.Copy).then_inc(s_cT, 1)

            def expert_silu(j, k):
                e = (k - 1) % NX
                act.wait_ge(e_g, NX * j + k + 1)
                wait(act, e_hu, NX * j + k - 1)
                act.activation(s_act[:, k % 2], bG[:], ACT.Silu, bias=b13[:, 0, e:e + 1]).then_inc(e_s, 1)

            def split_h(j, k):
                i = len(SPLIT) * j + SPLIT.index(k)
                if k == 0:
                    act.wait_ge(e_hu, NX * j + 1)
                else:
                    act.wait_ge(e_h, NE * j + k)
                if i >= 2:
                    act.wait_ge(e_y, NX * ((i - 2) // len(SPLIT)) + SPLIT[(i - 2) % len(SPLIT)] + 1)
                act.activation(h_h[:, i % 2], h[:, k % 3], ACT.Copy).then_inc(e_hh, 1)

            def split_w2():
                act.wait_ge(ld_w2, 16)
                act.activation(w2_h[:].rearrange("p e d -> p (e d)"),
                               w2_sb[:].rearrange("p e d -> p (e d)"), ACT.Copy).then_inc(c_w2h, 1)

            def split_w_in():
                act.wait_ge(ld_win, 16)
                act.activation(win_h[:], win_raw[:], ACT.Copy).then_inc(c_winh, 1)

            def split_w_dt():
                act.wait_ge(ld_wdt, 16)
                act.activation(wdt_h[:], wdt_raw[:], ACT.Copy).then_inc(c_wdth, 1)

            def split_w13():
                act.wait_ge(ld_w13, 16)
                act.activation(w13_h[:].rearrange("p a e d -> p (a e d)"),
                               w13_raw[:].rearrange("p a e d -> p (a e d)"), ACT.Copy).then_inc(c_w13h, 1)

            def copy_pick():
                act.wait_ge(c_pickraw, 2)
                act.activation(pick[:].rearrange("p e d -> p (e d)"),
                               pick_raw[:].rearrange("p e d -> p (e d)"), ACT.Copy).then_inc(c_pick, 1)

            def split_b2():
                act.wait_ge(ld_b2, 16)
                act.activation(b2_hl[:], b2_raw[:], ACT.Copy).then_inc(c_b2h, 1)

            do = once()
            split_w_in()
            do(split_x, 0)
            do(split_x, 1)
            do(middle_tap, 0, 0)
            do(middle_tap, 0, 1)
            do(silu_z_c, 0)
            split_w_dt()
            do(silu_conv, 0, 0)
            do(silu_conv, 0, 1)
            do(middle_tap, 1, 0)
            do(middle_tap, 1, 1)
            do(silu_z_a, 0)
            split_w13()
            do(silu_z_a, 1)
            do(silu_conv, 1, 0)
            do(softplus_parts, 0, 0)
            do(silu_z_c, 1)
            do(silu_conv, 1, 1)
            do(softplus_parts, 0, 1)
            load_ln_exp()
            do(softplus_exp, 0, 0)
            do(softplus_exp, 0, 1)
            do(softplus_ln, 0, 0)
            do(softplus_ln, 0, 1)
            do(decay, 0, 0)
            do(split_x, 2)
            do(softplus_parts, 1, 0)
            do(decay, 0, 1)
            do(softplus_exp, 1, 0)
            do(softplus_ln, 1, 0)
            do(softplus_parts, 1, 1)
            do(softplus_exp, 1, 1)
            do(softplus_ln, 1, 1)
            do(decay, 1, 0)
            do(middle_tap, 2, 0)
            do(decay, 1, 1)
            do(middle_tap, 2, 1)
            do(silu_conv, 2, 0)
            do(silu_conv, 2, 1)
            split_b2()
            do(silu_z_c, 2)
            do(softplus_parts, 2, 0)
            do(split_x, 3)
            do(silu_z_a, 2)
            do(copy_x1, 0)
            do(softplus_parts, 2, 1)
            do(expert_silu, 0, 0)
            load_ln_exp()
            do(softplus_exp, 2, 0)
            do(split_x, 4)
            do(softplus_ln, 2, 0)
            do(exp_scores, 0)
            do(softplus_exp, 2, 1)
            do(softplus_ln, 2, 1)
            do(decay, 2, 0)
            copy_pick()
            do(decay, 2, 1)
            do(copy_weights, 0)
            do(middle_tap, 3, 0)
            for s in range(LEAD, NB + 6):
                do(decay, s - 1, 1)
                do(silu_z_a, s - 1)
                do(copy_weights, s - 3)
                do(middle_tap, s, 0)
                do(expert_silu, s - 3, 0)
                do(middle_tap, s, 1)
                do(expert_silu, s - 3, 1)
                do(copy_x1, s - 2)
                do(split_x, s + 1)
                do(expert_silu, s - 3, 2)
                do(silu_conv, s, 0)
                do(silu_z_c, s)
                do(silu_conv, s, 1)
                do(expert_silu, s - 3, 3)
                do(expert_silu, s - 3, 4)
                do(softplus_parts, s, 0)
                do(softplus_parts, s, 1)
                do(expert_silu, s - 3, 5)
                if s < NB:
                    load_ln_exp()
                do(softplus_exp, s, 0)
                do(softplus_exp, s, 1)
                do(softplus_ln, s, 0)
                do(softplus_ln, s, 1)
                do(exp_scores, s - 2)
                do(decay, s, 0)
                do(expert_silu, s - 3, 6)
                do(expert_silu, s - 3, 7)
                do(norm_sum, s - 4)
                do(expert_silu, s - 3, 8)

        @block.vector
        def _(dve):
            NS = 9

            def tap_before(j, t):
                n = rows[t]
                dve.wait_ge(f_raw, 2 * j + t + 1)
                wait(dve, f_sx, 2 * (j - 1) + t + 1)
                dve.scalar_tensor_tensor(out=conv[0:n, t], in0=craw[0:n, t, 0:T], scalar=cv[0:n, t, W0:W0 + 1],
                                         in1=tap[0:n, t], op0=ALU.mult, op1=ALU.add).then_inc(f_cv, 1)

            def tap_after(j, t):
                n = rows[t]
                dve.wait_ge(f_cv, 4 * j + 2 * t + 1)
                dve.scalar_tensor_tensor(out=conv[0:n, t], in0=craw[0:n, t, 2:T + 2],
                                         scalar=cv[0:n, t, W2:W2 + 1], in1=conv[0:n, t],
                                         op0=ALU.mult, op1=ALU.add).then_inc(f_cv, 1)

            def low_conv_c(j):
                p = j % 2
                dve.wait_ge(f_sx, 2 * j + 2)
                wait(dve, f_dtm, 2 * (j - 1))
                dve.tensor_tensor(xc_h[CR:2 * CR, p, 1], xconv[0:CR, p, 1], xc_h[0:CR, p, 1].bitcast(F32),
                                  ALU.subtract).then_inc(f_lowC, 1)

            def add_softplus(j, t):
                p = j % 2
                n = rows[t]
                dve.wait_ge(f_L, 2 * j + t + 1)
                wait(dve, s_cs, 2 * (j - 2) + t + 1)
                dve.tensor_tensor(dt[0:n, p, t], pos[0:n, t], mag[0:n, t], ALU.add).then_inc(f_dt, 1)

            def cumulate(j, t):
                p, n = j % 2, rows[t]
                dve.wait_ge(s_g, 2 * j + t + 1)
                wait(dve, s_cs, 2 * (j - 1) + t + 1)
                wait(dve, s_y1, 2 * (j - 2) + t + 1)
                first = 0.0 if p == 0 else csum[0:n, 1 - p, t, T - 1:T]
                dve.tensor_tensor_scan(csum[0:n, p, t], dt[0:n, p, t], zeros[0:n], first,
                                       ALU.add, ALU.add).then_inc(s_cs, 1)

            def add_skip(j, t):
                p, n = j % 2, rows[t]
                dve.wait_ge(s_y1, 2 * j + t + 1)
                dve.scalar_tensor_tensor(out=ae[0:n, p, t], in0=xconv[0:n, p, t], scalar=cv[0:n, t, DP:DP + 1],
                                         in1=ae[0:n, p, t], op0=ALU.mult, op1=ALU.add).then_inc(s_y2, 1)

            def add_x(j):
                p = j % 2
                dve.wait_ge(s_op, j + 1)
                dve.wait_ge(x_in[p], 16 * (j // 2 + 1))
                wait(dve, s_xt, j)
                r_flat = r[:].rearrange("p c d -> p (c d)")
                dve.tensor_tensor(r_flat, (bY if j == 0 else m1)[:], x_tm[:, p].rearrange("p c d -> p (c d)"),
                                  ALU.add).then_inc(s_r, 1)

            def x1_stats(j):
                dve.wait_ge(s_r, j + 1)
                for c in range(NCH):
                    last = dve.bn_stats(stats[:, c], r[:, c])
                last.then_inc(s_bn, 1)

            def x1_mean_var(j):
                dve.wait_ge(s_bn, j + 1)
                for c in range(NCH):
                    last = dve.bn_aggr(mv[:, c], stats[:, c])
                last.then_inc(s_mv, 1)

            def norm_x1(j, i):
                dve.wait_ge(s_rs, j + 1)
                for c in (2 * i, 2 * i + 1):
                    last = dve.tensor_scalar(r[:, c], r[:, c], mv[:, c, 0:1], rstd[:, c:c + 1],
                                             ALU.subtract, ALU.mult)
                if i == 1:
                    last.then_inc(s_x1, 1)

            flat = lambda t: t[:].rearrange("p c e -> p (c e)")

            def copy_scores(j):
                dve.wait_ge(s_lg, j + 1)
                dve.tensor_copy(flat(lg), m2[:, 0:NCH * NE]).then_inc(s_l, 1)

            def best_two(j):
                dve.wait_ge(s_l, j + 1)
                for c in range(NCH):
                    last = dve.max(top[:, c], lg[:, c])
                last.then_inc(s_gate, 1)

            def compare_scores(j):
                dve.wait_ge(s_gate, NS * j + 1)
                best = top[:, :, 0:1].broadcast_to([P, NCH, NE])
                second = top[:, :, 1:2].broadcast_to([P, NCH, NE])
                dve.tensor_tensor(shifted[:], lg[:], best, ALU.subtract).then_inc(s_d, 1)
                dve.tensor_tensor(above[:], lg[:], second, ALU.is_gt)
                dve.tensor_tensor(n_above[:], top[:, :, 0], top[:, :, 1], ALU.is_gt)
                dve.tensor_tensor(level[:], lg[:], second, ALU.is_equal).then_inc(s_gate, 1)

            def count_equal(j):
                dve.wait_ge(s_gate, NS * j + 2)
                dve.tensor_tensor_scan(flat(order), group_keep[:], flat(level), 0.0, ALU.mult, ALU.add).then_inc(s_gate, 1)

            def count_above(j):
                dve.wait_ge(s_gate, NS * j + 3)
                dve.tensor_tensor(order[:], order[:], n_above[:].unsqueeze(2).broadcast_to([P, NCH, NE]),
                                  ALU.add).then_inc(s_gate, 1)

            def keep_first(j):
                dve.wait_ge(s_gate, NS * j + 4)
                dve.scalar_tensor_tensor(out=flat(wanted), in0=flat(order), scalar=2.0, in1=flat(level),
                                         op0=ALU.is_le, op1=ALU.mult).then_inc(s_gate, 1)

            def choose(j):
                dve.wait_ge(s_gate, NS * j + 5)
                dve.tensor_tensor(wanted[:], wanted[:], above[:], ALU.add).then_inc(s_gate, 1)

            def weigh_exps(j):
                dve.wait_ge(s_ex, j + 1)
                dve.wait_ge(s_gate, NS * j + 6)
                dve.tensor_tensor(wanted[:], wanted[:], ex[:], ALU.mult)
                dve.tensor_reduce(den[:], ex[:], mybir.AxisListType.X, ALU.add).then_inc(s_gate, 1)

            def invert_total(j):
                dve.wait_ge(s_gate, NS * j + 7)
                dve.reciprocal(rden[:], den[:]).then_inc(s_gate, 1)

            def scale_weights(j):
                dve.wait_ge(s_gate, NS * j + 8)
                dve.tensor_tensor(wanted[:], wanted[:], rden[:].unsqueeze(2).broadcast_to([P, NCH, NE]),
                                  ALU.mult).then_inc(s_gate, 1)

            def weights_high(j):
                dve.wait_ge(s_gate, NS * j + 9)
                wait(dve, s_ct, j)
                high = comb[:, :, 0:2 * TOP].rearrange("p c (a e) -> p c a e", a=2)[:, :, :, 0:NE]
                dve.tensor_copy(high.bitcast(F32R),
                                wanted[:].unsqueeze(2).broadcast_to([P, NCH, 2, NE])).then_inc(s_ch, 1)

            def weights_low(j):
                dve.wait_ge(s_ch, j + 1)
                dve.tensor_tensor(comb[:, :, TOP + NE:TOP + 2 * NE].bitcast(F32R), wanted[:], comb[:, :, 0:NE],
                                  ALU.subtract).then_inc(s_cc, 1)

            def expert_gate(j, k):
                e = (k - 1) % NX
                dve.wait_ge(e_s, NX * j + k + 1)
                dve.wait_ge(e_u, NX * j + k + 1)
                if k == 0:
                    wait(dve, e_y, NX * j - 2)
                else:
                    wait(dve, e_h, NE * j + k - 2)
                dve.scalar_tensor_tensor(out=h[:, 0] if k == 0 else hu[:, k % 2], in0=bU[:],
                                         scalar=b13[:, 1, e:e + 1], in1=s_act[:, k % 2],
                                         op0=ALU.add, op1=ALU.mult).then_inc(e_hu, 1)

            def expert_weigh(j, k):
                dve.wait_ge(e_hu, NX * j + k + 1)
                dve.wait_ge(e_cb, NE * j + k)
                wait(dve, e_y, NX * j + k - 2)
                dve.tensor_tensor(h[:, k % 3], hu[:, k % 2], bC[:], ALU.mult).then_inc(e_h, 1)

            def add_x1(j):
                dve.wait_ge(e_yd, j + 1)
                wait(dve, n_t, j)
                dve.tensor_tensor(fin[:], bY[:], x1T[:, j % 2], ALU.add).then_inc(e_f, 1)

            def sum_stats(j):
                dve.wait_ge(n_t, j + 1)
                for c in range(NCH):
                    last = dve.bn_stats(stats2[:, c], m3[:, c * P:(c + 1) * P])
                last.then_inc(n_bn, 1)

            def sum_mean_var(j):
                dve.wait_ge(n_bn, j + 1)
                for c in range(NCH):
                    last = dve.bn_aggr(mv2[:, c], stats2[:, c])
                last.then_inc(n_mv, 1)

            def clear_buffers():
                dve.memset(y[CR:P, 1], 0.0)
                dve.memset(zeros[:], 0.0)
                dve.memset(comb[:], 0.0)
                dve.memset(group_keep[:], 1.0).then_inc(z_dve, 1)
                dve.wait_ge(z_dve, 1)
                dve.memset(group_keep[:, 0:NCH * NE:NE], 0.0)
                dve.memset(comb[:, :, NE:NX], 1.0)
                dve.memset(comb[:, :, TOP + 2 * NE:TOP + 2 * NE + 1], 1.0).then_inc(z_dve, 1)
                dve.wait_ge(z_dve, 2)

            def low_w_in():
                dve.wait_ge(c_winh, 1)
                dve.tensor_tensor(win_l[:], win_raw[:], win_h[:].bitcast(F32), ALU.subtract).then_inc(c_winl, 1)
                dve.wait_ge(ld_small, 16)

            def low_w_dt():
                dve.wait_ge(c_wdth, 1)
                dve.tensor_tensor(wdt_l[:], wdt_raw[:], wdt_h[:].bitcast(F32), ALU.subtract).then_inc(c_wdtl, 1)

            do = once()
            low_w_in()
            clear_buffers()
            do(tap_before, 0, 0)
            do(tap_after, 0, 0)
            do(tap_before, 0, 1)
            do(tap_after, 0, 1)
            do(tap_before, 1, 0)
            do(tap_after, 1, 0)
            low_w_dt()
            do(low_conv_c, 0)
            do(tap_before, 1, 1)
            do(tap_after, 1, 1)
            do(low_conv_c, 1)
            do(add_softplus, 0, 0)
            do(add_softplus, 0, 1)
            do(add_softplus, 1, 0)
            do(cumulate, 0, 0)
            do(cumulate, 0, 1)
            do(add_softplus, 1, 1)
            do(add_skip, 0, 0)
            do(tap_before, 2, 0)
            do(add_skip, 0, 1)
            do(tap_after, 2, 0)
            do(tap_before, 2, 1)
            do(tap_after, 2, 1)
            do(low_conv_c, 2)
            do(add_x, 0)
            do(x1_stats, 0)
            do(x1_mean_var, 0)
            do(norm_x1, 0, 0)
            do(norm_x1, 0, 1)
            do(cumulate, 1, 0)
            do(cumulate, 1, 1)
            do(add_skip, 1, 0)
            do(copy_scores, 0)
            do(add_skip, 1, 1)
            do(best_two, 0)
            do(compare_scores, 0)
            do(count_equal, 0)
            do(count_above, 0)
            do(keep_first, 0)
            do(choose, 0)
            do(weigh_exps, 0)
            do(expert_gate, 0, 0)
            do(add_softplus, 2, 0)
            do(invert_total, 0)
            do(add_softplus, 2, 1)
            do(scale_weights, 0)
            do(add_x, 1)
            do(x1_stats, 1)
            do(x1_mean_var, 1)
            do(weights_high, 0)
            do(weights_low, 0)
            do(norm_x1, 1, 0)
            do(norm_x1, 1, 1)
            for s in range(LEAD, NB + 6):
                do(norm_x1, s - 2, 1)
                do(add_x1, s - 4)
                do(tap_before, s, 0)
                do(cumulate, s - 1, 0)
                do(expert_gate, s - 3, 0)
                do(tap_after, s, 0)
                do(tap_before, s, 1)
                do(expert_gate, s - 3, 1)
                do(cumulate, s - 1, 1)
                do(tap_after, s, 1)
                do(expert_gate, s - 3, 2)
                do(expert_weigh, s - 3, 1)
                do(copy_scores, s - 2)
                do(low_conv_c, s)
                do(best_two, s - 2)
                do(expert_gate, s - 3, 3)
                do(expert_weigh, s - 3, 2)
                do(add_skip, s - 1, 0)
                do(add_skip, s - 1, 1)
                do(expert_weigh, s - 3, 3)
                do(expert_gate, s - 3, 4)
                do(compare_scores, s - 2)
                do(sum_stats, s - 4)
                do(count_equal, s - 2)
                do(expert_weigh, s - 3, 4)
                do(expert_gate, s - 3, 5)
                do(count_above, s - 2)
                do(sum_mean_var, s - 4)
                do(keep_first, s - 2)
                do(add_softplus, s, 0)
                do(choose, s - 2)
                do(expert_weigh, s - 3, 5)
                do(add_softplus, s, 1)
                do(weigh_exps, s - 2)
                do(expert_gate, s - 3, 6)
                do(add_x, s - 1)
                do(expert_weigh, s - 3, 6)
                do(invert_total, s - 2)
                do(scale_weights, s - 2)
                do(expert_gate, s - 3, 7)
                do(x1_stats, s - 1)
                do(expert_weigh, s - 3, 7)
                do(x1_mean_var, s - 1)
                do(weights_high, s - 2)
                do(expert_gate, s - 3, 8)
                do(weights_low, s - 2)
                do(expert_weigh, s - 3, 8)
                do(norm_x1, s - 1, 0)

        @block.gpsimd
        def _(pool):
            def low_x(j):
                p = j % 2
                pool.wait_ge(f_xh, j + 1)
                wait(pool, f_B, j - 1)
                pool.tensor_tensor(xl[:, p], xw[:, p], xh[:, p].bitcast(F32), ALU.subtract).then_inc(f_xl, 1)

            def low_conv_a(j):
                p = j % 2
                pool.wait_ge(f_sx, 2 * j + 1)
                wait(pool, f_dtm, 2 * j)
                pool.tensor_tensor(xc_l[:, p], xconv[:, p, 0], xc_h[:, p, 0].bitcast(F32),
                                   ALU.subtract).then_inc(f_lowA, 1)

            def weigh_dt(j, t):
                p, n = j % 2, rows[t]
                pool.wait_ge(f_ae, 2 * j + t + 1)
                pool.tensor_tensor(dt[0:n, p, t], dt[0:n, p, t], xconv[0:n, p, t], ALU.mult).then_inc(s_wd, 1)

            def weigh_decay(j, t):
                p, n = j % 2, rows[t]
                pool.wait_ge(s_wd, 2 * j + t + 1)
                pool.tensor_tensor(dt[0:n, p, t], dt[0:n, p, t], ae[0:n, p, t], ALU.mult).then_inc(s_g, 1)

            def decay_csum(j, t):
                p, n = j % 2, rows[t]
                pool.wait_ge(s_cs, 2 * j + t + 1)
                pool.tensor_tensor(ae[0:n, p, t], csum[0:n, p, t], ae[0:n, p, t], ALU.mult).then_inc(s_y1, 1)

            def gate_z(j, t):
                p, n = j % 2, rows[t]
                pool.wait_ge(s_y2, 2 * j + t + 1)
                pool.wait_ge(f_szA, j + 1)
                wait(pool, s_op, j)
                if j == 0:
                    pool.wait_ge(z_dve, 1)
                pool.tensor_tensor(y[0:n, t], ae[0:n, p, t], sz[0:n, p, t], ALU.mult).then_inc(s_y, 1)

            def x1_eps(j):
                pool.wait_ge(s_mv, j + 1)
                pool.tensor_scalar(ve[:], mv[:, :, 1], EPS, 1.0, ALU.add, ALU.mult).then_inc(s_ve, 1)

            def x1_inv_std(j):
                pool.wait_ge(s_ve, j + 1)
                pool.tensor_tensor(rstd[:], ve[:], minus_half[:], ALU.pow).then_inc(s_rs, 1)

            def sum_eps(j):
                pool.wait_ge(n_mv, j + 1)
                pool.tensor_scalar(ve2[:], mv2[:, :, 1], EPS, 1.0, ALU.add, ALU.mult)
                pool.tensor_scalar(neg_mean[:], mv2[:, :, 0], -1.0, 1.0, ALU.mult, ALU.mult).then_inc(n_ve, 1)

            def sum_inv_std(j):
                pool.wait_ge(n_ve, j + 1)
                pool.tensor_tensor(rstd2[:], ve2[:], minus_half[:], ALU.pow).then_inc(n_rs, 1)

            def sum_shift(j):
                pool.wait_ge(n_rs, j + 1)
                pool.tensor_tensor(shift2[:], neg_mean[:], rstd2[:], ALU.mult).then_inc(n_sh, 1)

            def low_x1(j):
                p = j % 2
                pool.wait_ge(s_x1h, j + 1)
                wait(pool, e_yd, j - 1)
                pool.tensor_tensor(x1l[:, p], x1T[:, p], x1h[:, p].bitcast(F32), ALU.subtract).then_inc(s_x1l, 1)

            def low_h(j, k):
                i = len(SPLIT) * j + SPLIT.index(k)
                pool.wait_ge(e_hh, i + 1)
                pool.tensor_tensor(h_l[:, i % 2], h[:, k % 3], h_h[:, i % 2].bitcast(F32),
                                   ALU.subtract).then_inc(e_hl, 1)

            def low_w2():
                pool.wait_ge(c_w2h, 1)
                pool.tensor_tensor(w2_l[:].rearrange("p e d -> p (e d)"), w2_sb[:].rearrange("p e d -> p (e d)"),
                                   w2_h[:].bitcast(F32).rearrange("p e d -> p (e d)"),
                                   ALU.subtract).then_inc(c_w2l, 1)

            def low_w13():
                pool.wait_ge(c_w13h, 1)
                pool.tensor_tensor(w13_l[:].rearrange("p a e d -> p (a e d)"),
                                   w13_raw[:].rearrange("p a e d -> p (a e d)"),
                                   w13_h[:].bitcast(F32).rearrange("p a e d -> p (a e d)"),
                                   ALU.subtract).then_inc(c_w13l, 1)

            def low_b2():
                pool.wait_ge(c_b2h, 1)
                pool.tensor_tensor(b2_hl[0:NX, :], b2_raw[0:NX, :], b2_hl[0:NX, :].bitcast(F32),
                                   ALU.subtract).then_inc(c_b2l, 1)

            def build_identity():
                pool.memset(xw[:, :, 0:T + 2:T + 1], 0.0).then_inc(z_window, 1)
                pool.memset(ident[:], 0.0)
                pool.memset(pick_raw[:], 0.0)
                pool.memset(minus_half[:], -0.5).then_inc(z_pool, 1)
                pool.wait_ge(z_pool, 1)
                pool.affine_select(out=ident[:], in_=ident[:], compare_op=ALU.not_equal, fill=1.0, base=0,
                                   pattern=[[-1, P]], channel_multiplier=1).then_inc(c_ident, 1)
                pool.affine_select(out=pick_raw[:], in_=pick_raw[:], compare_op=ALU.not_equal, fill=1.0, base=-TOP,
                                   pattern=[[-1, NE], [0, P]], channel_multiplier=1).then_inc(c_pickraw, 1)

            def build_pick():
                pool.wait_ge(c_pickraw, 1)
                pool.affine_select(out=pick_raw[:], in_=pick_raw[:], compare_op=ALU.not_equal, fill=1.0, base=-TOP - NE,
                                   pattern=[[-1, NE], [0, P]], channel_multiplier=1).then_inc(c_pickraw, 1)

            do = once()
            build_identity()
            do(low_x, 0)
            do(low_x, 1)
            do(low_conv_a, 0)
            build_pick()
            do(low_conv_a, 1)
            low_w13()
            do(weigh_dt, 0, 0)
            do(low_x, 2)
            do(weigh_dt, 0, 1)
            do(weigh_decay, 0, 0)
            do(weigh_decay, 0, 1)
            do(decay_csum, 0, 0)
            do(decay_csum, 0, 1)
            do(gate_z, 0, 0)
            do(weigh_dt, 1, 0)
            do(gate_z, 0, 1)
            do(low_conv_a, 2)
            do(weigh_decay, 1, 0)
            do(weigh_dt, 1, 1)
            do(x1_eps, 0)
            do(x1_inv_std, 0)
            do(weigh_decay, 1, 1)
            do(low_x1, 0)
            do(decay_csum, 1, 0)
            do(decay_csum, 1, 1)
            do(gate_z, 1, 0)
            do(gate_z, 1, 1)
            do(low_x, 3)
            do(x1_eps, 1)
            do(x1_inv_std, 1)
            low_b2()
            do(weigh_dt, 2, 0)
            do(weigh_decay, 2, 0)
            for s in range(LEAD, NB + 6):
                do(weigh_dt, s - 1, 1)
                do(weigh_decay, s - 1, 1)
                do(low_conv_a, s)
                do(decay_csum, s - 1, 0)
                do(low_x, s + 1)
                do(decay_csum, s - 1, 1)
                do(gate_z, s - 1, 0)
                do(gate_z, s - 1, 1)
                do(low_x1, s - 2)
                do(sum_eps, s - 4)
                do(sum_inv_std, s - 4)
                do(sum_shift, s - 4)
                do(x1_eps, s - 1)
                do(x1_inv_std, s - 1)
                do(weigh_dt, s, 0)
                do(weigh_decay, s, 0)

def kernel(**inputs):
    import concourse.bacc as bacc
    from concourse.bass_utils import run_bass_kernel_spmd

    i = {k.replace("L0_", ""): np.asarray(v) for k, v in inputs.items()}
    B, L, D = i["attn_x"].shape
    DI = i["attn_W_out"].shape[1]
    x = i["attn_x"].reshape(B * L, D)
    w_in = i["attn_W_in"]
    w_in = np.concatenate([w_in[:P], w_in[P:DI], w_in[DI + P:], w_in[DI:DI + P]])

    def pad(a, n=P, axis=0):
        return np.concatenate([a, np.zeros_like(a, shape=(n - a.shape[0], a.shape[1]) if axis == 0 else
                                                (a.shape[0], n - a.shape[1]))], axis)

    stack = lambda routed, shared: np.concatenate([i[routed], i[shared][None]]).swapaxes(0, 1)
    b2, sb2 = i["ffn_b2"], i["ffn_sb2"][None]
    w_dt, w_out = i["attn_dt_w"].T, i["attn_W_out"].T
    chan = np.stack([*i["attn_conv_w"][:, 0].T, i["attn_conv_b"], i["attn_dt_b"], i["attn_A"], i["attn_Dp"]], 1)
    arrays = {
        "x": x,
        "xT": x.T,
        "w_in": w_in.T,
        "small": np.concatenate([chan[:P], pad(chan[P:]), stack("ffn_b1", "ffn_sb1"), stack("ffn_b3", "ffn_sb3")], 1),
        "w_dt": np.concatenate([pad(w_dt[:P], 2 * P, 1), pad(np.concatenate([w_dt[P:], w_dt[P:]]), 2 * P, 1)], 1),
        "w_out_gate": np.concatenate([w_out[:P], pad(w_out[P:]), i["ffn_gate_w"].T], 1),
        "w13": np.concatenate([stack("ffn_w1", "ffn_sw1"), stack("ffn_w3", "ffn_sw3")], 1).reshape(P, -1),
        "w2": stack("ffn_w2", "ffn_sw2"),
        "b2": np.concatenate([pad(np.concatenate([b2, sb2]), TOP), pad(np.concatenate([b2, b2, sb2]), P - TOP)]),
    }
    arrays = {f"{k}_dram": np.ascontiguousarray(v) for k, v in arrays.items()}
    nc = bacc.Bacc("TRN2", target_bir_lowering=False, num_devices=1)
    args = [nc.dram_tensor(k, a.shape, mybir.dt.from_np(a.dtype), kind="ExternalInput").ap()
            for k, a in arrays.items()]
    out = nc.dram_tensor("out_dram", (B * L, D), F32, kind="ExternalOutput").ap()
    build(nc, *args, out)
    got = run_bass_kernel_spmd(nc, [arrays], core_ids=[0]).results[0]["out_dram"]
    return got.reshape(B, L, D)
```

```python
from contextlib import ExitStack

import numpy as np
import concourse.bass as bass
from concourse import mybir

ALU = mybir.AluOpType
ACT = mybir.ActivationFunctionType
F32 = mybir.dt.float32
F32R = mybir.dt.float32r

P = 128
T = 512
NCH = T // P
EPS = 1e-5
TOP, FULL = 32, 64
LEAD = 3
W0, W1, W2, CB, DTB, AC, DP = range(7)


def build(nc, x, xT, w_in, small, w_dt, w_out_gate, w13, w2, b2, out):
    tokens = x.shape[0]
    NB = tokens // T
    DI = w_in.shape[1] // 2
    CR = DI - P
    NX = w2.shape[1]
    NE = NX - 1
    rows = (P, CR)

    x_chunks = x.rearrange("(b c p) d -> b p c d", c=NCH, p=P)
    out_chunks = out.rearrange("(b c p) d -> b p c d", c=NCH, p=P)

    with ExitStack() as ctx:
        def sb(name, shape, dt=F32):
            return ctx.enter_context(nc.sbuf_tensor(name, shape, dt))

        def bank(name):
            return ctx.enter_context(nc.psum_tensor(name, [P, T], F32))

        def sem(name):
            return ctx.enter_context(nc.semaphore(name))

        win_raw = sb("win_raw", [P, 2 * DI])
        win_h, win_l = sb("win_h", [P, 2 * DI], F32R), sb("win_l", [P, 2 * DI], F32R)
        wdt_raw = sb("wdt_raw", [P, 2, 2 * P])
        wdt_h, wdt_l = sb("wdt_h", [P, 2, 2 * P], F32R), sb("wdt_l", [P, 2, 2 * P], F32R)
        wout_gate = sb("wout_gate", [P, 2 * P + NE])
        wout, wgate = wout_gate[:, 0:2 * P].rearrange("p (t d) -> p t d", t=2), wout_gate[:, 2 * P:]
        small_sb = sb("small_sb", [P, 2 * 7 + 2 * NX])
        cv = small_sb[:, 0:14].rearrange("p (t c) -> p t c", t=2)
        b13 = small_sb[:, 14:].rearrange("p (a e) -> p a e", a=2)
        w13_raw = sb("w13_raw", [P, 2, NX, P])
        w13_h, w13_l = sb("w13_h", [P, 2, NX, P], F32R), sb("w13_l", [P, 2, NX, P], F32R)
        w2_sb = sb("w2_sb", [P, NX, P])
        b2_raw = sb("b2_raw", [P, P])
        b2_hl = sb("b2_hl", [P, P], F32R)
        ident = sb("ident", [P, P])
        zeros = sb("zeros", [P, 1])
        group_keep = sb("group_keep", [P, NCH * NE])
        minus_half = sb("minus_half", [P, NCH])
        w2_h, w2_l = sb("w2_h", [P, NX, P], F32R), sb("w2_l", [P, NX, P], F32R)

        xw = sb("xw", [P, 2, T + 2])
        xh, xl = sb("xh", [P, 2, T + 2], F32R), sb("xl", [P, 2, T + 2], F32R)
        edge = sb("edge", [P, 2, 2])
        conv = sb("conv", [P, 2, 2, T])
        xconv = sb("xconv", [P, 2, 2, T])
        sz = sb("sz", [P, 2, 2, T])
        xc_h = sb("xc_h", [P, 2, 2, T], F32R)
        xc_l = sb("xc_l", [P, 2, T], F32R)
        mag = sb("mag", [P, 2, T])
        pos = sb("pos", [P, 2, T])
        dt = sb("dt", [P, 2, 2, T])
        ae = sb("ae", [P, 2, 2, T])
        x_tm = sb("x_tm", [P, 2, NCH, P])
        csum = sb("csum", [P, 2, 2, T])
        y = sb("y", [P, 2, T])
        r = sb("r", [P, NCH, P])
        stats = sb("stats", [P, NCH, 6])
        mv = sb("mv", [P, NCH, 2])
        ve = sb("ve", [P, NCH])
        rstd = sb("rstd", [P, NCH])
        x1T = sb("x1T", [P, 2, T])
        x1h, x1l = sb("x1h", [P, 2, T], F32R), sb("x1l", [P, 2, T], F32R)
        lg = sb("lg", [P, NCH, NE])
        top = sb("top", [P, NCH, 8])
        shifted = sb("shifted", [P, NCH, NE])
        ex = sb("ex", [P, NCH, NE])
        above, level, order, wanted = (sb(n, [P, NCH, NE]) for n in ("above", "level", "order", "wanted"))
        n_above = sb("n_above", [P, NCH])
        den, rden = sb("den", [P, NCH]), sb("rden", [P, NCH])
        comb = sb("comb", [P, NCH, P])
        cT = sb("cT", [P, 2, T], F32R)
        c_rows = sb("c_rows", [P, T])
        c_all = sb("c_all", [P, NE, T])
        w13_flat = w13_raw[:].rearrange("p a e d -> p (a e d)")
        s_act = w13_flat[:, 0:2 * T].rearrange("p (a t) -> p a t", a=2)
        hu = w13_flat[:, 2 * T:4 * T].rearrange("p (a t) -> p a t", a=2)
        h = sb("h", [P, 3, T])
        h_h, h_l = sb("h_h", [P, 2, T], F32R), sb("h_l", [P, 2, T], F32R)
        fin = wdt_raw[:].rearrange("p a d -> p (a d)")
        stats2 = sb("stats2", [P, NCH, 6])
        mv2 = sb("mv2", [P, NCH, 2])
        ve2 = sb("ve2", [P, NCH])
        rstd2 = sb("rstd2", [P, NCH])
        neg_mean = sb("neg_mean", [P, NCH])
        shift2 = sb("shift2", [P, NCH])
        o_tm = sb("o_tm", [P, NCH, P])

        bG, bY, m0, m1, m2, m3 = (bank(n) for n in ("bG", "bY", "m0", "m1", "m2", "m3"))
        bU = [bank("bU0"), bank("bU1")]
        c_dram = nc.dram_tensor("c_dram", (2, NE, T), F32, kind="Internal").ap()

        win_loaded, small_loaded, wdt_loaded, wout_loaded = sem("win_loaded"), sem("small_loaded"), sem("wdt_loaded"), sem("wout_loaded")
        w13_loaded, w2_loaded, b2_loaded, window_cleared = sem("w13_loaded"), sem("w2_loaded"), sem("b2_loaded"), sem("window_cleared")
        pool_cleared, dve_cleared, ident_built, win_high = sem("pool_cleared"), sem("dve_cleared"), sem("ident_built"), sem("win_high")
        win_low, wdt_high, wdt_low, w13_high = sem("win_low"), sem("wdt_high"), sem("wdt_low"), sem("w13_high")
        w13_low, b2_high, b2_low, w2_high = sem("w13_low"), sem("b2_high"), sem("b2_low"), sem("w2_high")
        w2_low = sem("w2_low")
        x_high, x_low, projected, halo_projected = sem("x_high"), sem("x_low"), sem("projected"), sem("halo_projected")
        taps_out, convolved, conv_silu_done, conv_low_a = sem("taps_out"), sem("convolved"), sem("conv_silu_done"), sem("conv_low_a")
        conv_low_c, z_projected, z_silu_c, z_silu_a = sem("conv_low_c"), sem("z_projected"), sem("z_silu_c"), sem("z_silu_a")
        dt_multiplied, dt_parts_out, exp_done, ln_done = sem("dt_multiplied"), sem("dt_parts_out"), sem("exp_done"), sem("ln_done")
        dt_done, decay_done = sem("dt_done"), sem("decay_done")
        dt_weighed, terms_ready, summed, sum_decayed = sem("dt_weighed"), sem("terms_ready"), sem("summed"), sem("sum_decayed")
        skip_added, y_ready, first_c_steps, out_projected = sem("skip_added"), sem("y_ready"), sem("first_c_steps"), sem("out_projected")
        residual_added, x1_sums_done, x1_mean_ready, x1_var_ready = sem("residual_added"), sem("x1_sums_done"), sem("x1_mean_ready"), sem("x1_var_ready")
        x1_rstd_ready = sem("x1_rstd_ready")
        x1_ready, x1_turned, x1_high, x1_low = sem("x1_ready"), sem("x1_turned"), sem("x1_high"), sem("x1_low")
        scores_ready, scores_copied, shifted_ready, exps_ready = sem("scores_ready"), sem("scores_copied"), sem("shifted_ready"), sem("exps_ready")
        routing_steps, weights_split, weights_ready, weights_turned = sem("routing_steps"), sem("weights_split"), sem("weights_ready"), sem("weights_turned")
        weights_copied, weight_rows_copied, weights_saved = sem("weights_copied"), sem("weight_rows_copied"), sem("weights_saved")
        g_ready, u_ready, g_silu_done, gated = sem("g_ready"), sem("u_ready"), sem("g_silu_done"), sem("gated")
        hidden_ready, hidden_high, hidden_low, layer_2_done = sem("hidden_ready"), sem("hidden_high"), sem("hidden_low"), sem("layer_2_done")
        experts_summed = sem("experts_summed")
        fin_ready, fin_turned, fin_sums_done, fin_mean_ready = sem("fin_ready"), sem("fin_turned"), sem("fin_sums_done"), sem("fin_mean_ready")
        fin_var_ready, fin_rstd_ready, fin_shift_ready, out_ready = sem("fin_var_ready"), sem("fin_rstd_ready"), sem("fin_shift_ready"), sem("out_ready")
        window_loaded, x_loaded = [sem("window_loaded0"), sem("window_loaded1")], [sem("x_loaded0"), sem("x_loaded1")]
        weights_in = [sem(f"weights_in{e}") for e in range(NE)]
        stored = sem("stored")

        def wait(eng, s, v):
            if not (isinstance(v, int) and v <= 0):
                eng.wait_ge(s, v)

        PARTS_FROM, PARTS_TO = NB - 4, 7

        def in_parts(j, k):
            return j >= PARTS_FROM and k < PARTS_TO

        def n_parts(j, k):
            return (j - PARTS_FROM) * PARTS_TO + k + 1

        def by_pool(j, t):
            return 1 if j == 0 else 2 * j + t

        block = ctx.enter_context(nc.Block())

        @block.sync
        def _(sp):
            sp.dma_start(win_raw[:], w_in).then_inc(win_loaded, 16)

            def load_window(j):
                p = j % 2
                wait(sp, x_low, j - 1)
                if j == 0 or j == 1:
                    sp.wait_ge(window_cleared, 1)
                if p == 0:
                    dst, src = xw[:, p, 1:T + 2], xT[:, j * T:(j + 1) * T + 1]
                else:
                    dst, src = xw[:, p, 0:T + 1], xT[:, j * T - 1:(j + 1) * T]
                sp.dma_start(dst, src).then_inc(window_loaded[p], 16)

            load_window(0)
            sp.dma_start(small_sb[:], small).then_inc(small_loaded, 16)
            sp.dma_start(wdt_raw[:].rearrange("p t d -> p (t d)"), w_dt).then_inc(wdt_loaded, 16)
            load_window(1)
            sp.dma_start(w13_raw[:].rearrange("p a e d -> p (a e d)"), w13).then_inc(w13_loaded, 16)
            sp.dma_start(wout_gate[:], w_out_gate).then_inc(wout_loaded, 16)
            for j in range(2):
                sp.dma_start(x_tm[:, j], x_chunks[j]).then_inc(x_loaded[j], 16)
            sp.dma_start(w2_sb[:], w2).then_inc(w2_loaded, 16)
            sp.dma_start(b2_raw[:], b2).then_inc(b2_loaded, 16)

            def share_weights(j):
                sp.wait_ge(weight_rows_copied, j + 1)
                wait(sp, hidden_ready, NE * (j - 1))
                sp.dma_start(c_dram[j % 2], c_rows[FULL:FULL + NE, :]).then_inc(weights_saved, 16)
                sp.wait_ge(weights_saved, 16 * (j + 1))
                for e in range(NE):
                    wait(sp, hidden_ready, NE * (j - 1) + e + 1)
                    sp.dma_start(c_all[:, e], c_dram[j % 2, e:e + 1].broadcast_to([P, T])).then_inc(weights_in[e], 16)

            for s in range(NB + 4):
                j = s + 2
                if j < NB:
                    load_window(j)
                j = s + 1
                if 2 <= j < NB:
                    wait(sp, residual_added, j - 1)
                    sp.dma_start(x_tm[:, j % 2], x_chunks[j]).then_inc(x_loaded[j % 2], 16)
                if 0 <= s - 2 < NB:
                    share_weights(s - 2)
                j = s - 4
                if j >= 0:
                    sp.wait_ge(out_ready, j + 1)
                    sp.dma_start(out_chunks[j], o_tm[:]).then_inc(stored, 16)
            sp.wait_ge(stored, 16 * NB)

        def once(later=()):
            ran = {}

            def do(piece, j, *which):
                if ran.get((piece, which), int(piece in later and which == (1,))) == j < NB:
                    piece(j, *which)
                    ran[piece, which] = j + 1
            return do

        @block.tensor
        def _(pe):
            def mm3(dst, wh, wl, mh, ml, start=True, stop=True):
                pe.matmul(dst, wh, mh, start=start, stop=False)
                pe.matmul(dst, wh, ml, start=False, stop=False)
                return pe.matmul(dst, wl, mh, start=False, stop=stop)

            through = dict.fromkeys(("project_in", "outer", "project_z", "project_dt", "project_out",
                                     "turn_x1", "score_experts", "turn_weights", "turn_sum"), 0)

            def project_in(j):
                p = j % 2
                if j == 0:
                    pe.wait_ge(win_low, 1)
                pe.wait_ge(x_low, j + 1)
                A, C = (bG, bU[0]) if j == 1 else (m0, m1)
                for t, dst in ((0, A), (1, C)):
                    if j != 1:
                        wait(pe, dt_parts_out, 2 * (through["project_dt"] - 1) + t + 1)
                        if t == 1:
                            wait(pe, residual_added, through["project_out"])
                    c = slice(t * P, (t + 1) * P)
                    mm3(dst[:], win_h[:, c], win_l[:, c], xh[:, p, 1:T + 1], xl[:, p, 1:T + 1]).then_inc(projected, 1)
                if j != 1:
                    through["project_in"] = j + 1
                if p == 0:
                    wait(pe, z_silu_a, through["project_z"])
                    wait(pe, scores_copied, through["score_experts"])
                    for t in range(2):
                        c = slice(t * P, (t + 1) * P)
                        last = mm3(m2[:, 2 * t:2 * t + 2], win_h[:, c], win_l[:, c],
                                   xh[:, p, 0:T + 2:T + 1], xl[:, p, 0:T + 2:T + 1])
                    last.then_inc(halo_projected, 1)
                    through["outer"] = j + 1

            def project_z(j):
                p = j % 2
                if j != 1:
                    wait(pe, scores_copied, through["score_experts"])
                if j % 2 == 0:
                    pe.wait_ge(convolved, 6 * j + 6)
                c = slice(2 * P, 3 * P)
                mm3((bU[1] if j == 1 else m2)[:], win_h[:, c], win_l[:, c],
                    xh[:, p, 1:T + 1], xl[:, p, 1:T + 1]).then_inc(z_projected, 1)
                if j != 1:
                    through["project_z"] = j + 1

            def project_dt(j):
                p = j % 2
                if j == 0:
                    pe.wait_ge(wdt_low, 1)
                pe.wait_ge(conv_silu_done, 2 * j + 2)
                pe.wait_ge(conv_low_a, j + 1)
                pe.wait_ge(conv_low_c, j + 1)
                pe.wait_ge(z_silu_c, j + 1)
                if j != 1:
                    wait(pe, residual_added, through["project_out"])
                for t, dst in ((0, bG if j == 1 else m0), (1, bU[0] if j == 1 else m1)):
                    c = slice(t * P, (t + 1) * P)
                    mm3(dst[:], wdt_h[:, 0, c], wdt_l[:, 0, c], xc_h[:, p, 0], xc_l[:, p], stop=False)
                    pe.matmul(dst[:], wdt_h[:, 1, c], xc_h[:, p, 1], start=False, stop=False)
                    pe.matmul(dst[:], wdt_l[:, 1, c], xc_h[:, p, 1], start=False, stop=True).then_inc(dt_multiplied, 1)
                if j != 1:
                    through["project_dt"] = j + 1

            def project_out(j):
                pe.wait_ge(y_ready, by_pool(j, 1))
                if j == 0:
                    pe.wait_ge(first_c_steps, 4)
                dst = bY if j == 0 else m1
                if j > 0:
                    wait(pe, dt_parts_out, 2 * through["project_dt"])
                    wait(pe, z_silu_c, through["project_in"])
                if j == 0:
                    pe.wait_ge(wout_loaded, 16)
                for c in range(NCH):
                    k = slice(c * P, (c + 1) * P)
                    pe.matmul(dst[:, k], y[:, 0, k], wout[:, 0, :], start=True, stop=False)
                    last = pe.matmul(dst[:, k], y[:, 1, k], wout[:, 1, :], start=False, stop=True)
                last.then_inc(out_projected, 1)
                if j > 0:
                    through["project_out"] = j + 1

            def m3_free():
                wait(pe, x1_high, through["turn_x1"])
                wait(pe, weights_copied, through["turn_weights"])
                wait(pe, out_ready, through["turn_sum"])

            def turn_x1(j):
                pe.wait_ge(x1_ready, j + 1)
                m3_free()
                for c in range(NCH):
                    k = slice(c * P, (c + 1) * P)
                    last = pe.transpose(m3[:, k], r[:, c, :], ident[:])
                last.then_inc(x1_turned, 1)
                through["turn_x1"] = j + 1

            def score_experts(j):
                p = j % 2
                pe.wait_ge(x1_high, j + 1)
                wait(pe, convolved, 6 * through["outer"])
                pe.wait_ge(z_silu_a, through["project_z"])
                wait(pe, scores_copied, j)
                for c in range(NCH):
                    last = pe.matmul(m2[:, c * NE:(c + 1) * NE], x1T[:, p, c * P:(c + 1) * P], wgate,
                                     start=True, stop=True)
                last.then_inc(scores_ready, 1)
                through["score_experts"] = j + 1

            def turn_weights(j):
                pe.wait_ge(weights_ready, j + 1)
                m3_free()
                for c in range(NCH):
                    k = slice(c * P, (c + 1) * P)
                    last = pe.transpose(m3[:, k], comb[:, c, :], ident[:])
                last.then_inc(weights_turned, 1)
                through["turn_weights"] = j + 1

            def expert_g(j, k):
                p = j % 2
                e = (k - 1) % NX
                if j == 0 and k == 0:
                    pe.wait_ge(w13_low, 1)
                    pe.wait_ge(dt_parts_out, 4)
                    pe.wait_ge(z_silu_a, 2)
                if k == 0:
                    pe.wait_ge(x1_low, j + 1)
                wait(pe, g_silu_done, NX * j + k)
                mm3(bG[:], w13_h[:, 0, e], w13_l[:, 0, e], x1h[:, p], x1l[:, p]).then_inc(g_ready, 1)

            def expert_u(j, k):
                p = j % 2
                e = (k - 1) % NX
                i = NX * j + k
                wait(pe, gated, i - 1)
                mm3(bU[i % 2][:], w13_h[:, 1, e], w13_l[:, 1, e], x1h[:, p], x1l[:, p]).then_inc(u_ready, 1)

            def expert_down(j, k):
                e = (k - 1) % NX
                if k == 0:
                    pe.wait_ge(gated, NX * j + 1)
                    wait(pe, fin_ready, j)
                    if j == 0:
                        pe.wait_ge(w2_loaded, 16)
                        pe.wait_ge(residual_added, 1)
                if in_parts(j, k):
                    i = n_parts(j, k)
                    if i == 1:
                        pe.wait_ge(w2_low, 1)
                    pe.wait_ge(hidden_low, i)
                    mm3(bY[:], w2_h[:, e], w2_l[:, e], h_h[:, i % 2], h_l[:, i % 2],
                        start=(k == 0), stop=False).then_inc(layer_2_done, 1)
                else:
                    if k > 0:
                        pe.wait_ge(hidden_ready, NE * j + k)
                    pe.matmul(bY[:], w2_sb[:, e], h[:, k % 3], start=(k == 0), stop=False).then_inc(layer_2_done, 1)

            def add_biases(j):
                p = j % 2
                pe.wait_ge(weights_copied, j + 1)
                if j == 0:
                    pe.wait_ge(b2_low, 1)
                pe.matmul(bY[:], b2_hl[:], cT[:, p], start=False, stop=True).then_inc(experts_summed, 1)

            def turn_sum(j):
                pe.wait_ge(fin_ready, j + 1)
                m3_free()
                for c in range(NCH):
                    k = slice(c * P, (c + 1) * P)
                    last = pe.transpose(m3[:, k], fin[:, k], ident[:])
                last.then_inc(fin_turned, 1)
                through["turn_sum"] = j + 1

            pe.wait_ge(ident_built, 1)
            do = once()
            do(project_in, 0)
            do(project_in, 1)
            do(project_z, 0)
            do(project_z, 1)
            do(project_dt, 0)
            do(project_in, 2)
            do(project_dt, 1)
            do(project_out, 0)
            do(project_z, 2)
            do(project_dt, 2)
            do(turn_x1, 0)
            do(score_experts, 0)
            do(expert_g, 0, 0)
            do(project_out, 1)
            do(project_in, 3)
            do(turn_weights, 0)
            do(expert_u, 0, 0)
            for s in range(LEAD, NB + 6):
                do(expert_g, s - 3, 0)
                do(expert_u, s - 3, 0)
                do(expert_g, s - 3, 1)
                do(turn_x1, s - 2)
                do(expert_u, s - 3, 1)
                do(expert_g, s - 3, 2)
                do(expert_u, s - 3, 2)
                do(turn_sum, s - 4)
                do(score_experts, s - 2)
                do(expert_g, s - 3, 3)
                do(expert_u, s - 3, 3)
                do(expert_down, s - 3, 0)
                do(expert_g, s - 3, 4)
                do(project_dt, s)
                do(expert_u, s - 3, 4)
                do(expert_g, s - 3, 5)
                do(expert_down, s - 3, 1)
                do(expert_u, s - 3, 5)
                do(expert_g, s - 3, 6)
                do(project_z, s)
                do(expert_u, s - 3, 6)
                do(project_out, s - 1)
                do(expert_down, s - 3, 2)
                do(expert_down, s - 3, 3)
                do(expert_g, s - 3, 7)
                do(expert_u, s - 3, 7)
                do(expert_down, s - 3, 4)
                do(expert_g, s - 3, 8)
                do(expert_u, s - 3, 8)
                do(expert_down, s - 3, 5)
                do(turn_weights, s - 2)
                do(expert_down, s - 3, 6)
                do(expert_down, s - 3, 7)
                do(expert_down, s - 3, 8)
                do(project_in, s + 1)
                do(add_biases, s - 3)

        @block.scalar
        def _(act):
            def split_x(j):
                p = j % 2
                act.wait_ge(window_loaded[p], 16 * (j // 2 + 1))
                wait(act, z_projected, j - 1)
                act.activation(xh[:, p], xw[:, p], ACT.Copy).then_inc(x_high, 1)

            def middle_tap(j, t):
                n = rows[t]
                src = ((bG, bU[0]) if j == 1 else (m0, m1))[t]
                if j == 0:
                    act.wait_ge(small_loaded, 16)
                act.wait_ge(projected, 2 * j + 1 + t)
                wait(act, conv_silu_done, 2 * (j - 2) + t + 1)
                done = act.activation(conv[0:n, j % 2, t], src[0:n, :], ACT.Identity, scale=cv[0:n, t, W1:W1 + 1],
                                      bias=cv[0:n, t, CB:CB + 1])
                if j % 2 == 0:
                    wait(act, convolved, 6 * (j - 3) + 3 * t + 3)
                    done = act.activation(edge[0:n, j // 2 % 2, t:t + 1], src[0:n, T - 1:T], ACT.Copy)
                done.then_inc(taps_out, 1)

            def silu_z_c(j):
                act.wait_ge(projected, 2 * j + 2)
                if j >= 2:
                    act.wait_ge(y_ready, by_pool(j - 2, 1))
                if j == 2:
                    act.wait_ge(first_c_steps, 4)
                act.activation(sz[0:CR, j % 2, 1], (bU[0] if j == 1 else m1)[CR:2 * CR, :], ACT.Silu).then_inc(z_silu_c, 1)

            def silu_conv(j, t):
                p, n = j % 2, rows[t]
                wait(act, dt_multiplied, 2 * (j - 1))
                wait(act, skip_added, 2 * (j - 2) + t + 1)
                act.wait_ge(convolved, 6 * j + 3 * t + 3)
                act.activation(xconv[0:n, p, t], conv[0:n, j % 2, t], ACT.Silu)
                act.activation(xc_h[0:n, p, t], conv[0:n, j % 2, t], ACT.Silu).then_inc(conv_silu_done, 1)

            def silu_z_a(j):
                act.wait_ge(z_projected, j + 1)
                if j >= 2:
                    act.wait_ge(y_ready, by_pool(j - 2, 0))
                act.activation(sz[:, j % 2, 0], (bU[1] if j == 1 else m2)[:], ACT.Silu).then_inc(z_silu_a, 1)

            def softplus_parts(j, t):
                src = (bG, bU[0])[t] if j == 1 else (m0, m1)[t]
                n, bias = rows[t], cv[0:rows[t], t, DTB:DTB + 1]
                act.wait_ge(dt_multiplied, 2 * j + t + 1)
                wait(act, dt_done, 2 * (j - 1) + t + 1)
                act.activation(mag[0:n, t], src[0:n, :], ACT.Abs, bias=bias)
                act.activation(pos[0:n, t], src[0:n, :], ACT.Relu, bias=bias).then_inc(dt_parts_out, 1)

            def load_ln_exp():
                act.preload_act_table_set("natural_log_exp_and_others")

            def softplus_exp(j, t):
                n = rows[t]
                act.wait_ge(dt_parts_out, 2 * j + t + 1)
                act.activation(mag[0:n, t], mag[0:n, t], ACT.Exp, scale=-1.0).then_inc(exp_done, 1)

            def softplus_ln(j, t):
                n = rows[t]
                act.wait_ge(exp_done, 2 * j + t + 1)
                act.activation(mag[0:n, t], mag[0:n, t], ACT.Ln, bias=1.0).then_inc(ln_done, 1)

            def decay(j, t):
                p = j % 2
                n = rows[t]
                act.wait_ge(dt_done, 2 * j + t + 1)
                if j >= 2:
                    act.wait_ge(y_ready, by_pool(j - 2, t))
                if j == 2 and t == 1:
                    act.wait_ge(first_c_steps, 4)
                act.activation(ae[0:n, p, t], dt[0:n, p, t], ACT.Exp,
                               scale=cv[0:n, t, AC:AC + 1]).then_inc(decay_done, 1)

            def exp_scores(j):
                act.wait_ge(shifted_ready, j + 1)
                act.activation(ex[:], shifted[:], ACT.Exp).then_inc(exps_ready, 1)

            def norm_sum(j):
                p = j % 2
                act.wait_ge(fin_shift_ready, j + 1)
                wait(act, stored, 16 * j)
                for c in range(NCH):
                    last = act.activation(o_tm[:, c], m3[:, c * P:(c + 1) * P], ACT.Identity,
                                          scale=rstd2[:, c:c + 1], bias=shift2[:, c:c + 1])
                last.then_inc(out_ready, 1)

            def copy_x1(j):
                p = j % 2
                act.wait_ge(x1_turned, j + 1)
                wait(act, fin_ready, j - 1)
                act.activation(x1T[:, p], m3[:], ACT.Copy)
                act.activation(x1h[:, p], m3[:], ACT.Copy).then_inc(x1_high, 1)

            def copy_weights(j):
                p = j % 2
                act.wait_ge(weights_turned, j + 1)
                wait(act, experts_summed, j - 1)
                wait(act, weights_saved, 16 * j)
                act.activation(c_rows[FULL:FULL + NE, :], m3[FULL:FULL + NE, :], ACT.Copy).then_inc(weight_rows_copied, 1)
                act.activation(cT[:, p], m3[:], ACT.Copy).then_inc(weights_copied, 1)

            def expert_silu(j, k):
                e = (k - 1) % NX
                act.wait_ge(g_ready, NX * j + k + 1)
                wait(act, gated, NX * j + k - 1)
                act.activation(s_act[:, k % 2], bG[:], ACT.Silu, bias=b13[:, 0, e:e + 1]).then_inc(g_silu_done, 1)

            def split_w_in():
                act.wait_ge(win_loaded, 16)
                act.activation(win_h[:], win_raw[:], ACT.Copy).then_inc(win_high, 1)

            def split_w_dt():
                act.wait_ge(wdt_loaded, 16)
                act.activation(wdt_h[:], wdt_raw[:], ACT.Copy).then_inc(wdt_high, 1)

            def split_h(j, k):
                if in_parts(j, k):
                    i = n_parts(j, k)
                    if k == 0:
                        act.wait_ge(gated, NX * j + 1)
                    else:
                        act.wait_ge(hidden_ready, NE * j + k)
                    if i > 2:
                        back = (j, k - 2) if k >= 2 else (j - 1, k - 2 + PARTS_TO)
                        act.wait_ge(layer_2_done, NX * back[0] + back[1] + 1)
                    act.activation(h_h[:, i % 2], h[:, k % 3], ACT.Copy).then_inc(hidden_high, 1)

            def split_b2():
                act.wait_ge(b2_loaded, 16)
                act.activation(b2_hl[:], b2_raw[:], ACT.Copy).then_inc(b2_high, 1)

            do = once()
            split_w_in()
            do(split_x, 0)
            split_w_dt()
            do(split_x, 1)
            do(middle_tap, 0, 0)
            do(middle_tap, 0, 1)
            do(silu_z_c, 0)
            do(silu_conv, 0, 0)
            do(middle_tap, 1, 0)
            do(silu_conv, 0, 1)
            do(split_x, 2)
            do(silu_z_c, 1)
            do(silu_z_a, 0)
            do(middle_tap, 1, 1)
            do(silu_z_a, 1)
            do(silu_conv, 1, 0)
            do(softplus_parts, 0, 0)
            do(silu_conv, 1, 1)
            do(softplus_parts, 0, 1)
            load_ln_exp()
            do(softplus_exp, 0, 0)
            do(softplus_ln, 0, 0)
            do(softplus_exp, 0, 1)
            do(middle_tap, 2, 0)
            do(softplus_ln, 0, 1)
            do(decay, 0, 0)
            do(decay, 0, 1)
            do(softplus_parts, 1, 0)
            do(softplus_parts, 1, 1)
            do(softplus_exp, 1, 0)
            do(softplus_ln, 1, 0)
            split_b2()
            do(softplus_exp, 1, 1)
            do(softplus_ln, 1, 1)
            do(decay, 1, 0)
            do(middle_tap, 2, 1)
            do(decay, 1, 1)
            do(silu_conv, 2, 0)
            do(silu_conv, 2, 1)
            do(silu_z_c, 2)
            do(split_x, 3)
            do(softplus_parts, 2, 0)
            do(silu_z_a, 2)
            do(copy_x1, 0)
            load_ln_exp()
            do(softplus_exp, 2, 0)
            do(softplus_parts, 2, 1)
            do(softplus_ln, 2, 0)
            do(softplus_exp, 2, 1)
            do(softplus_ln, 2, 1)
            do(decay, 2, 0)
            do(exp_scores, 0)
            do(split_x, 4)
            do(expert_silu, 0, 0)
            do(decay, 2, 1)
            do(middle_tap, 3, 0)
            do(copy_weights, 0)
            for s in range(LEAD, NB + 6):
                do(middle_tap, s, 1)
                do(expert_silu, s - 3, 0)
                do(silu_z_c, s)
                do(split_x, s + 1)
                do(expert_silu, s - 3, 1)
                do(copy_x1, s - 2)
                do(split_h, s - 3, 0)
                do(expert_silu, s - 3, 2)
                do(silu_conv, s, 0)
                do(silu_conv, s, 1)
                do(expert_silu, s - 3, 3)
                do(split_h, s - 3, 1)
                do(expert_silu, s - 3, 4)
                do(split_h, s - 3, 2)
                do(softplus_parts, s, 0)
                do(softplus_parts, s, 1)
                do(expert_silu, s - 3, 5)
                if s < NB:
                    load_ln_exp()
                do(softplus_exp, s, 0)
                do(split_h, s - 3, 3)
                do(softplus_ln, s, 0)
                do(softplus_exp, s, 1)
                do(exp_scores, s - 2)
                do(softplus_ln, s, 1)
                do(decay, s, 0)
                do(expert_silu, s - 3, 6)
                do(split_h, s - 3, 4)
                do(split_h, s - 3, 5)
                do(expert_silu, s - 3, 7)
                do(norm_sum, s - 4)
                do(split_h, s - 3, 6)
                do(expert_silu, s - 3, 8)
                do(decay, s, 1)
                do(copy_weights, s - 2)
                do(silu_z_a, s)
                do(middle_tap, s + 1, 0)

        @block.vector
        def _(dve):
            NS = 9

            def tap_before(j, t):
                n = rows[t]
                src = ((bG, bU[0]) if j == 1 else (m0, m1))[t]
                dve.wait_ge(taps_out, 2 * j + t + 1)
                dve.scalar_tensor_tensor(out=conv[0:n, j % 2, t, 1:T], in0=src[0:n, 0:T - 1], scalar=cv[0:n, t, W0:W0 + 1],
                                         in1=conv[0:n, j % 2, t, 1:T], op0=ALU.mult, op1=ALU.add).then_inc(convolved, 1)

            def tap_after(j, t):
                n = rows[t]
                src = ((bG, bU[0]) if j == 1 else (m0, m1))[t]
                dve.wait_ge(convolved, 6 * j + 3 * t + 1)
                dve.scalar_tensor_tensor(out=conv[0:n, j % 2, t, 0:T - 1], in0=src[0:n, 1:T], scalar=cv[0:n, t, W2:W2 + 1],
                                         in1=conv[0:n, j % 2, t, 0:T - 1], op0=ALU.mult, op1=ALU.add).then_inc(convolved, 1)

            def tap_outside(j, t):
                n = rows[t]
                dve.wait_ge(convolved, 6 * j + 3 * t + 2)
                if j % 2 == 0:
                    dve.wait_ge(halo_projected, j // 2 + 1)
                    at, outer, w = T - 1, m2[0:n, 2 * t + 1:2 * t + 2], W2
                else:
                    at, outer, w = 0, edge[0:n, j // 2 % 2, t:t + 1], W0
                dve.scalar_tensor_tensor(out=conv[0:n, j % 2, t, at:at + 1], in0=outer, scalar=cv[0:n, t, w:w + 1],
                                         in1=conv[0:n, j % 2, t, at:at + 1], op0=ALU.mult, op1=ALU.add).then_inc(convolved, 1)

            def low_conv_c(j):
                p = j % 2
                dve.wait_ge(conv_silu_done, 2 * j + 2)
                wait(dve, dt_multiplied, 2 * (j - 1))
                dve.tensor_tensor(xc_h[CR:2 * CR, p, 1], xconv[0:CR, p, 1], xc_h[0:CR, p, 1].bitcast(F32),
                                  ALU.subtract).then_inc(conv_low_c, 1)

            def add_softplus(j, t):
                p = j % 2
                n = rows[t]
                dve.wait_ge(ln_done, 2 * j + t + 1)
                wait(dve, summed, 2 * (j - 2) + t + 1)
                dve.tensor_tensor(dt[0:n, p, t], pos[0:n, t], mag[0:n, t], ALU.add).then_inc(dt_done, 1)

            def cumulate(j, t):
                p, n = j % 2, rows[t]
                if (j, t) == (0, 1):
                    dve.wait_ge(first_c_steps, 2)
                else:
                    dve.wait_ge(terms_ready, by_pool(j, t))
                wait(dve, summed, 2 * (j - 1) + t + 1)
                first = 0.0 if p == 0 else csum[0:n, 1 - p, t, T - 1:T]
                dve.tensor_tensor_scan(csum[0:n, p, t], dt[0:n, p, t], zeros[0:n, 0:1].broadcast_to([n, T]), first,
                                       ALU.add, ALU.add).then_inc(summed, 1)

            def add_skip(j, t):
                p, n = j % 2, rows[t]
                if (j, t) == (0, 1):
                    dve.wait_ge(first_c_steps, 3)
                else:
                    dve.wait_ge(sum_decayed, by_pool(j, t))
                dve.scalar_tensor_tensor(out=ae[0:n, p, t], in0=xconv[0:n, p, t], scalar=cv[0:n, t, DP:DP + 1],
                                         in1=ae[0:n, p, t], op0=ALU.mult, op1=ALU.add).then_inc(skip_added, 1)

            def add_x(j):
                p = j % 2
                dve.wait_ge(out_projected, j + 1)
                dve.wait_ge(x_loaded[p], 16 * (j // 2 + 1))
                wait(dve, x1_turned, j)
                r_flat = r[:].rearrange("p c d -> p (c d)")
                dve.tensor_tensor(r_flat, (bY if j == 0 else m1)[:], x_tm[:, p].rearrange("p c d -> p (c d)"),
                                  ALU.add).then_inc(residual_added, 1)

            def x1_stats(j):
                dve.wait_ge(residual_added, j + 1)
                for c in range(NCH):
                    last = dve.bn_stats(stats[:, c], r[:, c])
                last.then_inc(x1_sums_done, 1)

            def x1_mean_var(j):
                dve.wait_ge(x1_sums_done, j + 1)
                for c in range(NCH):
                    last = dve.bn_aggr(mv[:, c], stats[:, c])
                last.then_inc(x1_mean_ready, 1)

            def norm_x1(j, i):
                dve.wait_ge(x1_rstd_ready, j + 1)
                for c in (2 * i, 2 * i + 1):
                    last = dve.tensor_scalar(r[:, c], r[:, c], mv[:, c, 0:1], rstd[:, c:c + 1],
                                             ALU.subtract, ALU.mult)
                if i == 1:
                    last.then_inc(x1_ready, 1)

            flat = lambda t: t[:].rearrange("p c e -> p (c e)")

            def copy_scores(j):
                dve.wait_ge(scores_ready, j + 1)
                dve.tensor_copy(flat(lg), m2[:, 0:NCH * NE]).then_inc(scores_copied, 1)

            def best_two(j):
                dve.wait_ge(scores_copied, j + 1)
                for c in range(NCH):
                    last = dve.max(top[:, c], lg[:, c])
                last.then_inc(routing_steps, 1)

            def compare_scores(j):
                dve.wait_ge(routing_steps, NS * j + 1)
                best = top[:, :, 0:1].broadcast_to([P, NCH, NE])
                second = top[:, :, 1:2].broadcast_to([P, NCH, NE])
                dve.tensor_tensor(shifted[:], lg[:], best, ALU.subtract).then_inc(shifted_ready, 1)
                dve.tensor_tensor(above[:], lg[:], second, ALU.is_gt)
                dve.tensor_tensor(n_above[:], top[:, :, 0], top[:, :, 1], ALU.is_gt)
                dve.tensor_tensor(level[:], lg[:], second, ALU.is_equal).then_inc(routing_steps, 1)

            def count_equal(j):
                dve.wait_ge(routing_steps, NS * j + 2)
                dve.tensor_tensor_scan(flat(order), group_keep[:], flat(level), 0.0, ALU.mult, ALU.add).then_inc(routing_steps, 1)

            def count_above(j):
                dve.wait_ge(routing_steps, NS * j + 3)
                dve.tensor_tensor(order[:], order[:], n_above[:].unsqueeze(2).broadcast_to([P, NCH, NE]),
                                  ALU.add).then_inc(routing_steps, 1)

            def keep_first(j):
                dve.wait_ge(routing_steps, NS * j + 4)
                dve.scalar_tensor_tensor(out=flat(wanted), in0=flat(order), scalar=2.0, in1=flat(level),
                                         op0=ALU.is_le, op1=ALU.mult).then_inc(routing_steps, 1)

            def choose(j):
                dve.wait_ge(routing_steps, NS * j + 5)
                dve.tensor_tensor(wanted[:], wanted[:], above[:], ALU.add).then_inc(routing_steps, 1)

            def weigh_exps(j):
                dve.wait_ge(exps_ready, j + 1)
                dve.wait_ge(routing_steps, NS * j + 6)
                dve.tensor_tensor(wanted[:], wanted[:], ex[:], ALU.mult)
                dve.tensor_reduce(den[:], ex[:], mybir.AxisListType.X, ALU.add).then_inc(routing_steps, 1)

            def invert_total(j):
                dve.wait_ge(routing_steps, NS * j + 7)
                dve.reciprocal(rden[:], den[:]).then_inc(routing_steps, 1)

            def scale_weights(j):
                dve.wait_ge(routing_steps, NS * j + 8)
                dve.tensor_tensor(wanted[:], wanted[:], rden[:].unsqueeze(2).broadcast_to([P, NCH, NE]),
                                  ALU.mult).then_inc(routing_steps, 1)

            def weights_high(j):
                dve.wait_ge(routing_steps, NS * j + 9)
                wait(dve, weights_turned, j)
                dve.tensor_copy(comb[:, :, FULL:FULL + NE], wanted[:])
                high = comb[:, :, 0:2 * TOP].rearrange("p c (a e) -> p c a e", a=2)[:, :, :, 0:NE]
                dve.tensor_copy(high.bitcast(F32R),
                                wanted[:].unsqueeze(2).broadcast_to([P, NCH, 2, NE])).then_inc(weights_split, 1)

            def weights_low(j):
                dve.wait_ge(weights_split, j + 1)
                dve.tensor_tensor(comb[:, :, TOP + NE:TOP + 2 * NE].bitcast(F32R), wanted[:], comb[:, :, 0:NE],
                                  ALU.subtract).then_inc(weights_ready, 1)

            def expert_gate(j, k):
                e = (k - 1) % NX
                dve.wait_ge(g_silu_done, NX * j + k + 1)
                dve.wait_ge(u_ready, NX * j + k + 1)
                if k == 0:
                    wait(dve, layer_2_done, NX * j - 2)
                else:
                    wait(dve, hidden_ready, NE * j + k - 2)
                dve.scalar_tensor_tensor(out=h[:, 0] if k == 0 else hu[:, k % 2], in0=bU[(NX * j + k) % 2][:],
                                         scalar=b13[:, 1, e:e + 1], in1=s_act[:, k % 2],
                                         op0=ALU.add, op1=ALU.mult).then_inc(gated, 1)

            def expert_weigh(j, k):
                dve.wait_ge(gated, NX * j + k + 1)
                e = k - 1
                dve.wait_ge(weights_in[e], 16 * (j + 1))
                wait(dve, layer_2_done, NX * j + k - 2)
                dve.tensor_tensor(h[:, k % 3], hu[:, k % 2], c_all[:, e], ALU.mult).then_inc(hidden_ready, 1)

            def add_x1(j):
                dve.wait_ge(experts_summed, j + 1)
                wait(dve, fin_turned, j)
                dve.tensor_tensor(fin, bY[:], x1T[:, j % 2], ALU.add).then_inc(fin_ready, 1)

            def sum_stats(j):
                dve.wait_ge(fin_turned, j + 1)
                for c in range(NCH):
                    last = dve.bn_stats(stats2[:, c], m3[:, c * P:(c + 1) * P])
                last.then_inc(fin_sums_done, 1)

            def sum_mean_var(j):
                dve.wait_ge(fin_sums_done, j + 1)
                for c in range(NCH):
                    last = dve.bn_aggr(mv2[:, c], stats2[:, c])
                last.then_inc(fin_mean_ready, 1)


            def first_c_dt():
                dve.wait_ge(dt_done, 2)
                dve.tensor_tensor(csum[0:CR, 0, 1], dt[0:CR, 0, 1], xconv[0:CR, 0, 1], ALU.mult).then_inc(first_c_steps, 1)

            def first_c_decay():
                dve.wait_ge(first_c_steps, 1)
                dve.wait_ge(decay_done, 2)
                dve.tensor_tensor(dt[0:CR, 0, 1], csum[0:CR, 0, 1], ae[0:CR, 0, 1], ALU.mult).then_inc(first_c_steps, 1)

            def first_c_csum():
                dve.wait_ge(first_c_steps, 2)
                dve.wait_ge(summed, 2)
                dve.tensor_tensor(ae[0:CR, 0, 1], csum[0:CR, 0, 1], ae[0:CR, 0, 1], ALU.mult).then_inc(first_c_steps, 1)

            def first_c_z():
                dve.wait_ge(first_c_steps, 3)
                dve.wait_ge(skip_added, 2)
                dve.wait_ge(z_silu_c, 1)
                dve.tensor_tensor(y[0:CR, 1], ae[0:CR, 0, 1], sz[0:CR, 0, 1], ALU.mult).then_inc(first_c_steps, 1)

            def clear_buffers():
                dve.memset(y[CR:P, 1], 0.0)
                dve.memset(zeros[:], 0.0)
                dve.memset(comb[:], 0.0)
                dve.memset(group_keep[:], 1.0).then_inc(dve_cleared, 1)
                dve.wait_ge(dve_cleared, 1)
                dve.memset(group_keep[:, 0:NCH * NE:NE], 0.0)
                dve.memset(comb[:, :, NE:NX], 1.0)
                dve.memset(comb[:, :, TOP + 2 * NE:TOP + 2 * NE + 1], 1.0).then_inc(dve_cleared, 1)
                dve.wait_ge(dve_cleared, 2)

            def split_w13():
                dve.wait_ge(w13_loaded, 16)
                dve.tensor_copy(w13_h[:].rearrange("p a e d -> p (a e d)"),
                                 w13_raw[:].rearrange("p a e d -> p (a e d)")).then_inc(w13_high, 1)

            def split_w2(j):
                if j == PARTS_FROM - 1:
                    dve.wait_ge(w2_loaded, 16)
                    dve.tensor_copy(w2_h[:].rearrange("p e d -> p (e d)"),
                                     w2_sb[:].rearrange("p e d -> p (e d)")).then_inc(w2_high, 1)

            def low_w_in():
                dve.wait_ge(win_high, 1)
                dve.tensor_tensor(win_l[:], win_raw[:], win_h[:].bitcast(F32), ALU.subtract).then_inc(win_low, 1)
                dve.wait_ge(small_loaded, 16)

            def low_w_dt():
                dve.wait_ge(wdt_high, 1)
                dve.tensor_tensor(wdt_l[:], wdt_raw[:], wdt_h[:].bitcast(F32), ALU.subtract).then_inc(wdt_low, 1)

            do = once()
            low_w_in()
            clear_buffers()
            low_w_dt()
            do(tap_before, 0, 0)
            do(tap_after, 0, 0)
            do(tap_outside, 0, 0)
            do(tap_before, 0, 1)
            do(tap_after, 0, 1)
            do(tap_outside, 0, 1)
            split_w13()
            do(low_conv_c, 0)
            do(tap_before, 1, 0)
            do(tap_after, 1, 0)
            do(tap_outside, 1, 0)
            do(tap_before, 1, 1)
            do(tap_after, 1, 1)
            do(tap_outside, 1, 1)
            do(low_conv_c, 1)
            do(add_softplus, 0, 0)
            do(add_softplus, 0, 1)
            do(tap_before, 2, 0)
            first_c_dt()
            do(cumulate, 0, 0)
            first_c_decay()
            do(tap_after, 2, 0)
            do(cumulate, 0, 1)
            do(add_skip, 0, 0)
            first_c_csum()
            do(add_softplus, 1, 0)
            do(add_skip, 0, 1)
            do(add_softplus, 1, 1)
            first_c_z()
            do(tap_outside, 2, 0)
            do(tap_before, 2, 1)
            do(tap_after, 2, 1)
            do(tap_outside, 2, 1)
            do(cumulate, 1, 0)
            do(cumulate, 1, 1)
            do(low_conv_c, 2)
            do(add_x, 0)
            do(x1_stats, 0)
            do(x1_mean_var, 0)
            do(norm_x1, 0, 0)
            do(norm_x1, 0, 1)
            do(add_skip, 1, 0)
            do(add_skip, 1, 1)
            do(copy_scores, 0)
            do(best_two, 0)
            do(compare_scores, 0)
            do(count_equal, 0)
            do(count_above, 0)
            do(add_softplus, 2, 0)
            do(keep_first, 0)
            do(choose, 0)
            do(weigh_exps, 0)
            do(add_softplus, 2, 1)
            do(add_x, 1)
            do(invert_total, 0)
            do(x1_stats, 1)
            do(scale_weights, 0)
            do(x1_mean_var, 1)
            do(split_w2, 0)
            do(weights_high, 0)
            do(weights_low, 0)
            do(norm_x1, 1, 0)
            do(norm_x1, 1, 1)
            do(expert_gate, 0, 0)
            do(cumulate, 2, 0)
            do(tap_before, 3, 0)
            do(tap_after, 3, 0)
            for s in range(LEAD, NB + 6):
                do(tap_after, s, 0)
                do(tap_outside, s, 0)
                do(expert_gate, s - 3, 0)
                do(tap_before, s, 1)
                do(tap_after, s, 1)
                do(tap_outside, s, 1)
                do(expert_gate, s - 3, 1)
                do(add_skip, s - 1, 0)
                do(expert_weigh, s - 3, 1)
                do(cumulate, s - 1, 1)
                do(low_conv_c, s)
                do(expert_gate, s - 3, 2)
                do(expert_weigh, s - 3, 2)
                do(copy_scores, s - 2)
                do(best_two, s - 2)
                do(expert_gate, s - 3, 3)
                do(compare_scores, s - 2)
                do(expert_weigh, s - 3, 3)
                do(count_equal, s - 2)
                do(add_skip, s - 1, 1)
                do(count_above, s - 2)
                do(expert_gate, s - 3, 4)
                do(sum_stats, s - 4)
                do(keep_first, s - 2)
                do(sum_mean_var, s - 4)
                do(choose, s - 2)
                do(expert_weigh, s - 3, 4)
                do(add_softplus, s, 0)
                do(weigh_exps, s - 2)
                do(expert_gate, s - 3, 5)
                do(invert_total, s - 2)
                do(add_x, s - 1)
                do(expert_weigh, s - 3, 5)
                do(scale_weights, s - 2)
                do(expert_gate, s - 3, 6)
                do(weights_high, s - 2)
                do(x1_stats, s - 1)
                do(expert_weigh, s - 3, 6)
                do(weights_low, s - 2)
                do(add_softplus, s, 1)
                do(expert_gate, s - 3, 7)
                do(x1_mean_var, s - 1)
                do(expert_weigh, s - 3, 7)
                do(expert_gate, s - 3, 8)
                do(expert_weigh, s - 3, 8)
                do(norm_x1, s - 1, 0)
                do(split_w2, s - 2)
                do(cumulate, s, 0)
                do(norm_x1, s - 1, 1)
                do(add_x1, s - 3)
                do(tap_before, s + 1, 0)

        @block.gpsimd
        def _(pool):
            def low_x(j):
                p = j % 2
                pool.wait_ge(x_high, j + 1)
                wait(pool, z_projected, j - 1)
                pool.tensor_tensor(xl[:, p], xw[:, p], xh[:, p].bitcast(F32), ALU.subtract).then_inc(x_low, 1)

            def low_conv_a(j):
                p = j % 2
                pool.wait_ge(conv_silu_done, 2 * j + 1)
                wait(pool, dt_multiplied, 2 * j)
                pool.tensor_tensor(xc_l[:, p], xconv[:, p, 0], xc_h[:, p, 0].bitcast(F32),
                                   ALU.subtract).then_inc(conv_low_a, 1)

            def weigh_dt(j, t):
                p, n = j % 2, rows[t]
                pool.wait_ge(dt_done, 2 * j + t + 1)
                if j >= 1:
                    pool.wait_ge(summed, 2 * (j - 1) + t + 1)
                if j >= 2:
                    pool.wait_ge(sum_decayed, by_pool(j - 2, t))
                pool.tensor_tensor(csum[0:n, p, t], dt[0:n, p, t], xconv[0:n, p, t], ALU.mult).then_inc(dt_weighed, 1)

            def weigh_decay(j, t):
                p, n = j % 2, rows[t]
                pool.wait_ge(dt_weighed, by_pool(j, t))
                pool.wait_ge(decay_done, 2 * j + t + 1)
                pool.tensor_tensor(dt[0:n, p, t], csum[0:n, p, t], ae[0:n, p, t], ALU.mult).then_inc(terms_ready, 1)

            def decay_csum(j, t):
                p, n = j % 2, rows[t]
                pool.wait_ge(summed, 2 * j + t + 1)
                pool.tensor_tensor(ae[0:n, p, t], csum[0:n, p, t], ae[0:n, p, t], ALU.mult).then_inc(sum_decayed, 1)

            def gate_z(j, t):
                p, n = j % 2, rows[t]
                pool.wait_ge(skip_added, 2 * j + t + 1)
                pool.wait_ge(z_silu_a, j + 1)
                wait(pool, out_projected, j)
                pool.tensor_tensor(y[0:n, t], ae[0:n, p, t], sz[0:n, p, t], ALU.mult).then_inc(y_ready, 1)

            def x1_eps(j):
                pool.wait_ge(x1_mean_ready, j + 1)
                pool.tensor_scalar(ve[:], mv[:, :, 1], EPS, 1.0, ALU.add, ALU.mult).then_inc(x1_var_ready, 1)

            def x1_inv_std(j):
                pool.wait_ge(x1_var_ready, j + 1)
                pool.tensor_tensor(rstd[:], ve[:], minus_half[:], ALU.pow).then_inc(x1_rstd_ready, 1)

            def sum_eps(j):
                pool.wait_ge(fin_mean_ready, j + 1)
                pool.tensor_scalar(ve2[:], mv2[:, :, 1], EPS, 1.0, ALU.add, ALU.mult)
                pool.tensor_scalar(neg_mean[:], mv2[:, :, 0], -1.0, 1.0, ALU.mult, ALU.mult).then_inc(fin_var_ready, 1)

            def sum_inv_std(j):
                pool.wait_ge(fin_var_ready, j + 1)
                pool.tensor_tensor(rstd2[:], ve2[:], minus_half[:], ALU.pow).then_inc(fin_rstd_ready, 1)

            def sum_shift(j):
                pool.wait_ge(fin_rstd_ready, j + 1)
                pool.tensor_tensor(shift2[:], neg_mean[:], rstd2[:], ALU.mult).then_inc(fin_shift_ready, 1)

            def low_x1(j):
                p = j % 2
                pool.wait_ge(x1_high, j + 1)
                wait(pool, experts_summed, j - 1)
                pool.tensor_tensor(x1l[:, p], x1T[:, p], x1h[:, p].bitcast(F32), ALU.subtract).then_inc(x1_low, 1)

            def low_h(j, k):
                if in_parts(j, k):
                    i = n_parts(j, k)
                    pool.wait_ge(hidden_high, i)
                    pool.tensor_tensor(h_l[:, i % 2], h[:, k % 3], h_h[:, i % 2].bitcast(F32),
                                       ALU.subtract).then_inc(hidden_low, 1)

            def low_w2(j):
                if j == PARTS_FROM - 1:
                    pool.wait_ge(w2_high, 1)
                    pool.tensor_tensor(w2_l[:].rearrange("p e d -> p (e d)"), w2_sb[:].rearrange("p e d -> p (e d)"),
                                       w2_h[:].bitcast(F32).rearrange("p e d -> p (e d)"),
                                       ALU.subtract).then_inc(w2_low, 1)

            def low_w13():
                pool.wait_ge(w13_high, 1)
                pool.tensor_tensor(w13_l[:].rearrange("p a e d -> p (a e d)"),
                                   w13_raw[:].rearrange("p a e d -> p (a e d)"),
                                   w13_h[:].bitcast(F32).rearrange("p a e d -> p (a e d)"),
                                   ALU.subtract).then_inc(w13_low, 1)

            def low_b2():
                pool.wait_ge(b2_high, 1)
                pool.tensor_tensor(b2_hl[0:NX, :], b2_raw[0:NX, :], b2_hl[0:NX, :].bitcast(F32),
                                   ALU.subtract).then_inc(b2_low, 1)

            def build_identity():
                pool.memset(xw[:, :, 0:T + 2:T + 1], 0.0).then_inc(window_cleared, 1)
                pool.memset(ident[:], 0.0)
                pool.memset(minus_half[:], -0.5).then_inc(pool_cleared, 1)
                pool.wait_ge(pool_cleared, 1)
                pool.affine_select(out=ident[:], in_=ident[:], compare_op=ALU.not_equal, fill=1.0, base=0,
                                   pattern=[[-1, P]], channel_multiplier=1).then_inc(ident_built, 1)

            do = once(later=(weigh_dt, weigh_decay, decay_csum, gate_z))
            build_identity()
            do(low_x, 0)
            do(low_x, 1)
            do(low_conv_a, 0)
            do(low_x, 2)
            low_w13()
            do(low_conv_a, 1)
            do(weigh_dt, 0, 0)
            do(weigh_decay, 0, 0)
            do(decay_csum, 0, 0)
            do(gate_z, 0, 0)
            do(weigh_dt, 1, 0)
            do(weigh_dt, 1, 1)
            do(weigh_decay, 1, 0)
            do(weigh_decay, 1, 1)
            do(low_conv_a, 2)
            do(decay_csum, 1, 0)
            do(x1_eps, 0)
            do(x1_inv_std, 0)
            do(decay_csum, 1, 1)
            do(gate_z, 1, 0)
            do(low_x1, 0)
            do(gate_z, 1, 1)
            do(low_x, 3)
            do(weigh_dt, 2, 0)
            do(x1_eps, 1)
            do(x1_inv_std, 1)
            do(weigh_decay, 2, 0)
            do(decay_csum, 2, 0)
            low_b2()
            for s in range(LEAD, NB + 6):
                do(low_x1, s - 3)
                do(x1_eps, s - 2)
                do(x1_inv_std, s - 2)
                do(weigh_decay, s - 1, 0)
                do(weigh_dt, s - 1, 1)
                do(decay_csum, s - 1, 0)
                do(weigh_decay, s - 1, 1)
                do(low_w2, s - 4)
                do(low_h, s - 3, 0)
                do(low_conv_a, s)
                do(gate_z, s - 1, 0)
                do(decay_csum, s - 1, 1)
                do(low_h, s - 3, 1)
                do(gate_z, s - 1, 1)
                do(low_h, s - 3, 2)
                do(sum_eps, s - 4)
                do(low_h, s - 3, 3)
                do(low_x, s + 1)
                do(sum_inv_std, s - 4)
                do(sum_shift, s - 4)
                do(weigh_dt, s, 0)
                do(low_h, s - 3, 4)
                do(low_h, s - 3, 5)
                do(low_h, s - 3, 6)

def kernel(**inputs):
    import concourse.bacc as bacc
    from concourse.bass_utils import run_bass_kernel_spmd

    i = {k.replace("L0_", ""): np.asarray(v) for k, v in inputs.items()}
    B, L, D = i["attn_x"].shape
    DI = i["attn_W_out"].shape[1]
    x = i["attn_x"].reshape(B * L, D)
    w_in = i["attn_W_in"]
    w_in = np.concatenate([w_in[:P], w_in[P:DI], w_in[DI + P:], w_in[DI:DI + P]])

    def pad(a, n=P, axis=0):
        return np.concatenate([a, np.zeros_like(a, shape=(n - a.shape[0], a.shape[1]) if axis == 0 else
                                                (a.shape[0], n - a.shape[1]))], axis)

    stack = lambda routed, shared: np.concatenate([i[routed], i[shared][None]]).swapaxes(0, 1)
    b2, sb2 = i["ffn_b2"], i["ffn_sb2"][None]
    w_dt, w_out = i["attn_dt_w"].T, i["attn_W_out"].T
    chan = np.stack([*i["attn_conv_w"][:, 0].T, i["attn_conv_b"], i["attn_dt_b"], i["attn_A"], i["attn_Dp"]], 1)
    arrays = {
        "x": x,
        "xT": x.T,
        "w_in": w_in.T,
        "small": np.concatenate([chan[:P], pad(chan[P:]), stack("ffn_b1", "ffn_sb1"), stack("ffn_b3", "ffn_sb3")], 1),
        "w_dt": np.concatenate([pad(w_dt[:P], 2 * P, 1), pad(np.concatenate([w_dt[P:], w_dt[P:]]), 2 * P, 1)], 1),
        "w_out_gate": np.concatenate([w_out[:P], pad(w_out[P:]), i["ffn_gate_w"].T], 1),
        "w13": np.concatenate([stack("ffn_w1", "ffn_sw1"), stack("ffn_w3", "ffn_sw3")], 1).reshape(P, -1),
        "w2": stack("ffn_w2", "ffn_sw2"),
        "b2": np.concatenate([pad(np.concatenate([b2, sb2]), TOP), pad(np.concatenate([b2, b2, sb2]), P - TOP)]),
    }
    arrays = {f"{k}_dram": np.ascontiguousarray(v) for k, v in arrays.items()}
    nc = bacc.Bacc("TRN2", target_bir_lowering=False, num_devices=1)
    args = [nc.dram_tensor(k, a.shape, mybir.dt.from_np(a.dtype), kind="ExternalInput").ap()
            for k, a in arrays.items()]
    out = nc.dram_tensor("out_dram", (B * L, D), F32, kind="ExternalOutput").ap()
    build(nc, *args, out)
    got = run_bass_kernel_spmd(nc, [arrays], core_ids=[0]).results[0]["out_dram"]
    return got.reshape(B, L, D)
```
